# Optimizing a Trainium2 kernel written in Bass

```python
import numpy as np
import jax
import jax.numpy as jnp

def _softmax(x, axis=-1):
    return jax.nn.softmax(x, axis=axis)
def _gelu(x):
    return jax.nn.gelu(x, approximate=True)
def _silu(x):
    return jax.nn.silu(x)
def _sigmoid(x):
    return jax.nn.sigmoid(x)
def _layernorm(x, axis=-1, eps=1e-5):
    m = jnp.mean(x, axis=axis, keepdims=True)
    v = jnp.var(x, axis=axis, keepdims=True)
    return (x - m) / jnp.sqrt(v + eps)
def _scatter_add(tgt, idx, src, axis=0):
    return tgt.at[idx].add(src)
def _segment_sum(src, seg, n):
    return jax.ops.segment_sum(src, seg, n)

kernel_name = 'mk_conv_preact_d1_conv_nhwc768_28fe0a'

def setup_inputs(seed: int = 0):
    np.random.seed(seed)
    _w = jnp.asarray
    def _rec_inputs():
        import jax
        import jax.numpy as jnp
        _gk = jax.random.key(seed)
        x = -4.65e-05 + 0.9999 * jax.random.normal(jax.random.fold_in(_gk, 1), (16, 64, 64, 768), jnp.float32)
        return x
    x = _rec_inputs()
    def _L0_conv_setup():
        import jax, jax.numpy as jnp
        import numpy as np
        B, H, W, D, R, E, K = (16, 64, 64, 768, 16, 4, 3)

        def conv2d(x, w, b):
            y = jax.lax.conv_general_dilated(x, w, window_strides=(1, 1), padding='SAME', dimension_numbers=('NCHW', 'OIHW', 'NCHW'))
            return y + b[None, :, None, None]
        key = jax.random.key(seed)
        ks = jax.random.split(key, 6)
        return {'x': jax.random.normal(ks[0], (B, H, W, D), jnp.float32), 'conv1_w': jax.random.normal(ks[1], (R, D, 1, 1), jnp.float32) * 0.02, 'conv1_b': jnp.zeros((R,), jnp.float32), 'convl_w': jax.random.normal(ks[2], (R, R, K, K), jnp.float32) * 0.05, 'convl_b': jnp.zeros((R,), jnp.float32), 'conv2_w': jax.random.normal(ks[3], (D, R, 1, 1), jnp.float32) * 0.05, 'conv2_b': jnp.zeros((D,), jnp.float32), 'H_w': jax.random.normal(ks[4], (E, R), jnp.float32) * 0.1, 'H_b': jnp.zeros((E,), jnp.float32)}
    _L0_conv_all = _L0_conv_setup()
    _L0_conv_in = {k: v for k, v in _L0_conv_all.items() if k in ('conv1_w', 'conv1_b', 'convl_w', 'convl_b', 'conv2_w', 'conv2_b', 'H_w', 'H_b', )}
    del _L0_conv_all

    return {
        "x": x,
        "L0_conv_conv1_w": _L0_conv_in["conv1_w"],
        "L0_conv_conv1_b": _L0_conv_in["conv1_b"],
        "L0_conv_convl_w": _L0_conv_in["convl_w"],
        "L0_conv_convl_b": _L0_conv_in["convl_b"],
        "L0_conv_conv2_w": _L0_conv_in["conv2_w"],
        "L0_conv_conv2_b": _L0_conv_in["conv2_b"],
        "L0_conv_H_w": _L0_conv_in["H_w"],
        "L0_conv_H_b": _L0_conv_in["H_b"],
    }

def reference(x, L0_conv_conv1_w, L0_conv_conv1_b, L0_conv_convl_w, L0_conv_convl_b, L0_conv_conv2_w, L0_conv_conv2_b, L0_conv_H_w, L0_conv_H_b):
    import jax
    import jax.numpy as jnp
    def _L0_conv_ref(x, conv1_w, conv1_b, convl_w, convl_b, conv2_w, conv2_b, H_w, H_b):
        import jax, jax.numpy as jnp
        import numpy as np
        B, H, W, D, R, E, K = (16, 64, 64, 768, 16, 4, 3)

        def conv2d(x, w, b):
            y = jax.lax.conv_general_dilated(x, w, window_strides=(1, 1), padding='SAME', dimension_numbers=('NCHW', 'OIHW', 'NCHW'))
            return y + b[None, :, None, None]
        xc = jnp.transpose(x, (0, 3, 1, 2))
        xc = conv2d(xc, conv1_w, conv1_b)
        pooled = jnp.mean(xc, axis=(2, 3))
        h = pooled @ H_w.T + H_b
        top2 = jnp.argsort(-h, axis=1)[:, :2]
        mask = jnp.zeros(h.shape, dtype=bool).at[jnp.arange(h.shape[0])[:, None], top2].set(True)
        g = jax.nn.softmax(jnp.where(mask, h, -jnp.inf), axis=1)
        experts = []
        for i in range(E):
            f = 2 ** i
            up = jax.image.resize(xc, (xc.shape[0], xc.shape[1], xc.shape[2] * f, xc.shape[3] * f), method='bilinear', antialias=False)
            up = conv2d(up, convl_w, convl_b)
            down = jax.image.resize(up, xc.shape, method='bilinear', antialias=False)
            experts.append(down)
        Es = jnp.stack(experts)
        gw = jnp.reshape(g, (E, g.shape[0], 1, 1, 1))
        out = jnp.sum(Es * gw, axis=0)
        out = conv2d(out, conv2_w, conv2_b)
        return jnp.transpose(out, (0, 2, 3, 1))

    def _gn(v, G=32, eps=1e-5):
        B_, H_, W_, C_ = v.shape
        g = v.reshape(B_, H_, W_, G, C_ // G)
        m = jnp.mean(g, axis=(1, 2, 4), keepdims=True)
        s = jnp.var(g, axis=(1, 2, 4), keepdims=True)
        return ((g - m) / jnp.sqrt(s + eps)).reshape(v.shape)

    def _ln_c(v, eps=1e-6):
        m = jnp.mean(v, axis=-1, keepdims=True)
        s = jnp.var(v, axis=-1, keepdims=True)
        return (v - m) / jnp.sqrt(s + eps)

    def _ln_t(v, eps=1e-5):
        m = jnp.mean(v, axis=-1, keepdims=True)
        s = jnp.var(v, axis=-1, keepdims=True)
        return (v - m) / jnp.sqrt(s + eps)

    def _to_tokens(v):
        B_, H_, W_, C_ = v.shape
        return v.reshape(B_, H_ * W_, C_)
    def _from_tokens(t, like):
        return t.reshape(like.shape)

    x = x + _L0_conv_ref(_gn(x), L0_conv_conv1_w, L0_conv_conv1_b, L0_conv_convl_w, L0_conv_convl_b, L0_conv_conv2_w, L0_conv_conv2_b, L0_conv_H_w, L0_conv_H_b)
    return x


_drawn_inputs = setup_inputs


def setup_inputs(seed=0):
    import zlib

    import numpy as np

    out = dict(_drawn_inputs(seed))
    spreads = {'L0_conv_conv1_b': (0.0, 0.372),
     'L0_conv_convl_b': (0.0, 0.283),
     'L0_conv_conv2_b': (0.0, 0.1),
     'L0_conv_H_b': (0.0, 0.8)}
    factors = {'L0_conv_H_w': 8.0}
    for name, (base, spread) in spreads.items():
        noise = np.random.default_rng([zlib.crc32(name.encode()), seed]).standard_normal(out[name].shape)
        drawn = base * np.exp(spread * noise) if base else spread * noise
        out[name] = jnp.asarray(drawn.astype(out[name].dtype))
    for name, factor in factors.items():
        out[name] = (out[name] * factor).astype(out[name].dtype)
    return out
```

```python
from contextlib import ExitStack

import concourse.bass as bass
from concourse import mybir

F32 = mybir.dt.float32
F32R = mybir.dt.float32r
ALU = mybir.AluOpType
ACT = mybir.ActivationFunctionType
AX = mybir.AxisListType

P = 128
B, HH, WW, D = 16, 64, 64, 768
R, E = 16, 4
G = 32
CG = D // G
KB = D // P
NH = P // R
NB = HH // NH
PIX = NB * WW
QN = 4
TILES = HH * WW // P
SPS = TILES // QN
CHUNKS = SPS // 2
SLOTS = 12
LOW = 8
TURNS = 3
LOOPS = (B - 1) // TURNS
STEPS = CHUNKS * KB
XT = 3
LEAD = 3
GN_EPS = 1e-5
LEFT, MID, RIGHT, LEFT_EDGE, RIGHT_EDGE = range(5)
NT = 5
UP, HERE, DOWN, FROM_ABOVE, FROM_BELOW, TOP, BOTTOM = range(7)
MAT_ROW_TAP = [LEFT, MID, RIGHT, LEFT, RIGHT, LEFT_EDGE, RIGHT_EDGE]
SAME, ABOVE, BELOW, FIRST, LAST = range(5)
MAT_MASK = [SAME, SAME, SAME, ABOVE, BELOW, FIRST, LAST]


def resize_taps():
    coef = []
    for e in range(E):
        f = 2 ** e
        sampled = [0] if f == 1 else [f // 2 - 1, f // 2]
        of_expert = []
        for d in (-1, 0, 1):
            inner = {-1: 0.0, 0: 0.0, 1: 0.0}
            first = last = 0.0
            for k in sampled:
                at = (k + d + 0.5) / f - 0.5
                low = int(at // 1)
                for offset, part in ((low, 1 - (at - low)), (low + 1, at - low)):
                    part /= len(sampled)
                    if not part:
                        continue
                    inner[offset] += part
                    if k + d >= 0 and offset <= 0:
                        first += part
                    if k + d < f and offset >= 0:
                        last += part
            of_expert.append([inner[-1], inner[0], inner[1], first - inner[0], last - inner[0]])
        coef.append(of_expert)
    return coef


def slot_place(i):
    return (i // 2) % 2, 2 * (i // 4) + i % 2


def column_ranges(ax):
    return {LEFT: (slice(1, WW), slice(0, WW - 1)), MID: (slice(0, WW), slice(0, WW)),
            RIGHT: (slice(0, WW - 1), slice(1, WW)), LEFT_EDGE: (slice(0, 1), slice(0, 1)),
            RIGHT_EDGE: (slice(WW - 1, WW), slice(WW - 1, WW))}[ax]


def blk_ranges(m):
    return {UP: (slice(1, NB), slice(0, NB - 1)), HERE: (slice(0, NB), slice(0, NB)),
            DOWN: (slice(0, NB - 1), slice(1, NB)), FROM_ABOVE: (slice(0, 1), slice(NB - 1, NB)),
            FROM_BELOW: (slice(NB - 1, NB), slice(0, 1)), TOP: (slice(0, 1), slice(0, 1)),
            BOTTOM: (slice(NB - 1, NB), slice(NB - 1, NB))}[m]


CONV = [(HERE, MID)] + [(m, a) for m in range(7) for a in range(NT) if (m, a) != (HERE, MID)]


def program(nc, x, conv1_w, conv1_b, convl_w, convl_b, conv2_w, conv2_b, H_w, H_b, out):
    slots_of = "b (q p j bb) w c -> b p j (bb w) q c"
    x_v = x.rearrange(slots_of, q=QN, p=2, j=4, bb=2)
    out_v = out.rearrange(slots_of, q=QN, p=2, j=4, bb=2)
    coef = resize_taps()

    ctx = ExitStack()
    scratch = ExitStack()
    with ctx:
        def sb(name, shape, dt=F32, stack=ctx):
            return stack.enter_context(nc.sbuf_tensor(name, shape, dt))

        def sem(name):
            return ctx.enter_context(nc.semaphore(name))

        x_low = sb("x_low", [P, LOW, QN, D])
        xc = sb("xc", [P, B, PIX])
        ident = sb("ident", [P, P])
        masks = sb("masks", [P, 5, NH, R])
        experts = sb("experts", [P, E, NT, NT, R])
        pooled = sb("pooled", [P, B])
        gates = sb("gates", [P, B, E])
        bias_l = sb("bias_l", [P, 1])
        bias_es = sb("bias_es", [P, B])
        small = sb("small", [P, 2, G])
        x_high = sb("x_high", [P, SLOTS - LOW, QN, D], stack=scratch)
        xT = sb("xT", [P, XT, QN, 2 * P], stack=scratch)
        w1T = sb("w1T", [P, KB, R], stack=scratch)
        w1 = sb("w1", [P, KB, 2, 2 * R], stack=scratch)
        group_sum = sb("group_sum", [P, G], stack=scratch)
        group_of = sb("group_of", [P, KB, G], stack=scratch)
        stats = sb("stats", [P, CHUNKS, G, 6], stack=scratch)
        moments = sb("moments", [P, CHUNKS, 2, G, 2], stack=scratch)
        ones = sb("ones", [P, P], stack=scratch)
        norm = sb("norm", [P, 6, G], stack=scratch)
        picked = sb("picked", [P, KB, G], stack=scratch)
        of_channel = sb("of_channel", [P, KB], stack=scratch)
        bias_1 = sb("bias_1", [P, 2], stack=scratch)
        sums = sb("sums", [P, 2], stack=scratch)
        gate_w = sb("gate_w", [P, E], stack=scratch)
        gate_b = sb("gate_b", [R, E], stack=scratch)
        w1_rep, other = (x_high[:, SLOTS - LOW - 1, i, :] for i in range(2))
        wl_raw = other[:, 0:R * 9].rearrange("p (o k) -> p o k", k=9)
        rows_of = other[:, R * 9:R * 9 + NT * 3 * R].rearrange("p (a d o) -> p a d o", a=NT, d=3)
        gate = x_high[0:B, 0, 0, 0:8 * E].rearrange("b (i e) -> b i e", i=8)
        gate_diag = x_high[0:B, 0, 1, 0:B * E].rearrange("b (s e) -> b s e", s=B)
        scratch.close()
        taps = sb("taps", [P, NT, NT, R])
        band = sb("band", [P, 7, NT, NH, R])
        es_hi = sb("es_hi", [P, PIX], F32R)
        es_lo = sb("es_lo", [P, PIX], F32R)
        es4 = sb("es4", [P, QN, PIX], F32R)
        spread = sb("spread", [P, QN, 2, P], F32R)
        w2 = sb("w2", [P, 2, D], F32R)
        b2 = sb("b2", [P, D], F32R)
        all_one = sb("all_one", [P, P], F32R)
        w2_raw = sb("w2_raw", [P, KB, R])
        row_kind = sb("row_kind", [P, 4])
        w2_rep = sb("w2_rep", [P, KB, P])
        w2_hi = sb("w2_hi", [P, D], F32R)
        w2_lo = sb("w2_lo", [P, D])
        b2_raw = sb("b2_raw", [P, D])

        xT_ps = ctx.enter_context(nc.psum_tensor("xT_ps", [P, XT, QN, 2 * P], F32))
        img_ps = ctx.enter_context(nc.psum_tensor("img_ps", [P, PIX], F32))
        misc_ps = ctx.enter_context(nc.psum_tensor("misc_ps", [P, 512], F32))
        flat_ps = xT_ps[:, :, :, :].rearrange("p n q c -> p n (q c)")
        add_ps = flat_ps[:, 0:2, 0:D]
        spread_ps = flat_ps[:, 2, :].rearrange("p (n c) -> p n c", n=2)
        img_v = img_ps[:, :].rearrange("p (k w) -> p k w", w=WW)
        xc_v = xc[:, :, :].rearrange("p b (k w) -> p b k w", w=WW)

        def slot(n):
            return x_low[:, n] if n < LOW else x_high[:, n - LOW]

        def chunk(n):
            half = x_low[:, n:n + 2] if n < LOW else x_high[:, n - LOW:n - LOW + 2]
            return half.rearrange("p s q c -> p (s q) c")

        loaded = [sem(f"loaded{n}") for n in range(SLOTS)]
        weights_in = sem("weights_in")
        consts_ready = sem("consts_ready")
        weights_ready = sem("weights_ready")
        w1_in_psum = sem("w1_in_psum")
        raw_used = sem("raw_used")
        stats_taken = sem("stats_taken")
        transposed = sem("transposed")
        xT_copied = sem("xT_copied")
        projected = sem("projected")
        moments_summed = sem("moments_summed")
        variance_ready = sem("variance_ready")
        deviation_ready = sem("deviation_ready")
        w1_ready = sem("w1_ready")
        xc_copied = sem("xc_copied")
        vector_step = sem("vector_step")
        pool_step = sem("pool_step")
        logits_done = sem("logits_done")
        logits_max = sem("logits_max")
        logits_exp = sem("logits_exp")
        gates_spread = sem("gates_spread")
        gate_rows = sem("gate_rows")
        gates_ready = sem("gates_ready")
        w2_in = sem("w2_in")
        w2_replicated = sem("w2_replicated")
        w2_transposed = sem("w2_transposed")
        w2_ready = sem("w2_ready")
        high_free = sem("high_free")
        taps_ready = sem("taps_ready")
        band_ready = sem("band_ready")
        conv_done = sem("conv_done")
        hi_ready = sem("hi_ready")
        lo_ready = sem("lo_ready")
        spread_done = sem("spread_done")
        es4_ready = sem("es4_ready")
        expanded = sem("expanded")
        added = sem("added")
        stored = [sem(f"stored{n}") for n in range(LOW)]

        block = ctx.enter_context(nc.Block())

        @block.sync
        def _(sp):
            def load(sample, i, n):
                p, j = slot_place(i)
                sp.dma_start(slot(n), x_v[sample, p, j]).then_inc(loaded[n], 16)

            def load_sample(loop, turn, first):
                for i in range(SPS):
                    at = SPS * turn + i
                    if not (first and at < SLOTS):
                        if i % 2 == 0:
                            last = (at - SLOTS) // 2 + 1
                            sp.wait_ge(transposed, loop * (TURNS * STEPS) + last * KB)
                    if first and at == SLOTS - 1:
                        sp.wait_ge(raw_used, 1)
                    load(loop * TURNS + turn, i, at % SLOTS)

            for turn in range(TURNS):
                load_sample(0, turn, True)
            with sp.Fori(1, LOOPS) as loop:
                for turn in range(TURNS):
                    load_sample(loop, turn, False)
            load_sample(LOOPS, 0, False)

            def store(order, sample, i):
                p, j = slot_place(i)
                sp.wait_ge(added, order * TILES + (i + 1) * QN)
                sp.dma_start(out_v[sample, p, j], slot(i)).then_inc(stored[i], 16)

            def reload(order, sample, i):
                sp.wait_ge(stored[i], order * 16 + 16)
                load(sample, i, i)

            def store_and_reload(order, sample, following):
                for i in range(SPS):
                    store(order, sample, i)
                    if i >= 2:
                        reload(order, following, i - 2)
                for i in (SPS - 2, SPS - 1):
                    reload(order, following, i)

            store_and_reload(0, B - 1, 0)
            with sp.Fori(1, B - 1) as order:
                store_and_reload(order, order - 1, order)
            for i in range(SPS):
                store(B - 1, B - 2, i)
            for i in range(SPS):
                sp.wait_ge(stored[i], 16 * B)

        @block.gpsimd
        def _(pool):
            done = [0]

            def link(ins):
                done[0] += 1
                ins.then_inc(pool_step, 1)
                pool.wait_ge(pool_step, done[0])

            wl_v = convl_w.rearrange("o i y x -> i o (y x)")
            w1_v = conv1_w.rearrange("r c y x -> r (c y x)")
            for h in range(NH):
                rows = slice(R * h, R * h + R)
                pool.dma_start(w1_rep[rows, :], w1_v).then_inc(weights_in, 16)
                pool.dma_start(wl_raw[rows, :, :], wl_v).then_inc(weights_in, 16)
                pool.dma_start(bias_l[rows, :], convl_b.unsqueeze(1)).then_inc(weights_in, 16)
                pool.dma_start(bias_1[rows, 0:1], conv1_b.unsqueeze(1)).then_inc(weights_in, 16)
                pool.dma_start(gate_w[rows, :], H_w.rearrange("e r -> r e"),
                               allow_slow_non_contiguous=True).then_inc(weights_in, 16)
            pool.dma_start(gate_b[:, :], H_b.partition_broadcast(R)).then_inc(weights_in, 16)

            link(nc.gpsimd.memset(ident[:, :], 0.0))
            link(nc.gpsimd.affine_select(out=ident[:, :], in_=ident[:, :], compare_op=ALU.not_equal, fill=1.0,
                                         base=0, pattern=[[-1, P]], channel_multiplier=1))
            link(nc.gpsimd.memset(group_of[:, :, :], 1.0))
            link(nc.gpsimd.affine_select(out=group_of[:, :, :], in_=group_of[:, :, :], compare_op=ALU.is_ge, fill=0.0,
                                         base=0, pattern=[[P, KB], [-CG, G]], channel_multiplier=1))
            link(nc.gpsimd.affine_select(out=group_of[:, :, :], in_=group_of[:, :, :], compare_op=ALU.is_ge, fill=0.0,
                                         base=CG - 1, pattern=[[-P, KB], [CG, G]], channel_multiplier=-1))
            link(nc.gpsimd.memset(masks[:, :, :, :], 1.0))
            for kind, shift in ((SAME, 0), (ABOVE, -1), (BELOW, 1), (FIRST, 0), (LAST, 0)):
                m = masks[:, kind]
                link(nc.gpsimd.affine_select(out=m, in_=m, compare_op=ALU.is_ge, fill=0.0, base=-R * shift,
                                             pattern=[[-R, NH], [0, R]], channel_multiplier=1))
                link(nc.gpsimd.affine_select(out=m, in_=m, compare_op=ALU.is_ge, fill=0.0, base=R * shift + R - 1,
                                             pattern=[[R, NH], [0, R]], channel_multiplier=-1))
            link(nc.gpsimd.memset(masks[:, FIRST, 1:NH], 0.0))
            link(nc.gpsimd.memset(masks[:, LAST, 0:NH - 1], 0.0))
            link(nc.gpsimd.memset(ones[:, :], 1.0 / (P * CHUNKS * 2)))
            nc.gpsimd.memset(w1[:, :, :, :], 0.0).then_inc(consts_ready, 1)

            pool.wait_ge(high_free, 1)
            pool.dma_start(w2_raw[:, :, :], conv2_w.rearrange("(k c) r y x -> c k (r y x)", k=KB)).then_inc(w2_in, 16)
            link(nc.gpsimd.memset(b2_raw[:, :], 0.0))
            for row in (0, 32):
                pool.dma_start(b2_raw[row:row + 1, :], conv2_b.unsqueeze(0)).then_inc(w2_in, 16)

            def bands(order):
                pool.wait_ge(taps_ready, order + 1)
                for m in range(7):
                    full = [P, NT, NH, R]
                    ins = nc.gpsimd.tensor_tensor(
                        out=band[:, m], in0=taps[:, MAT_ROW_TAP[m]].unsqueeze(2).broadcast_to(full),
                        in1=masks[:, MAT_MASK[m]].unsqueeze(1).broadcast_to(full), op=ALU.mult)
                ins.then_inc(band_ready, 1)

            bands(0)
            with pool.Fori(0, B - 1) as order:
                pool.wait_ge(conv_done, order + 1)
                bands(order + 1)

        @block.tensor
        def _(pe):
            pe.wait_ge(consts_ready, 1)
            pe.wait_ge(weights_in, (5 * NH + 1) * 16)
            for k in range(KB):
                last = nc.tensor.transpose(flat_ps[:, 0, k * P:(k + 1) * P], w1_rep[:, k * P:(k + 1) * P], ident[:, :])
            last.then_inc(w1_in_psum, 1)
            pe.wait_ge(weights_ready, 1)

            def transpose_step(loop, turn, step):
                c, k = divmod(step, KB)
                n = turn * STEPS + step
                buf = n % XT
                if k == 0:
                    for s in (2 * c, 2 * c + 1):
                        at = SPS * turn + s
                        pe.wait_ge(loaded[at % SLOTS], loop * 32 + (at // SLOTS + 1) * 16)
                if not (isinstance(loop, int) and loop == 0 and n < XT):
                    pe.wait_ge(xT_copied, loop * (TURNS * STEPS) + n - XT + 1)
                for q in range(QN):
                    for half in range(2):
                        last = nc.tensor.transpose(
                            xT_ps[:, buf, q, half * P:(half + 1) * P],
                            slot((SPS * turn + 2 * c + half) % SLOTS)[:, q, k * P:(k + 1) * P], ident[:, :])
                last.then_inc(transposed, 1)

            def project_step(loop, turn, step):
                c, k = divmod(step, KB)
                n = turn * STEPS + step
                pe.wait_ge(xT_copied, loop * (TURNS * STEPS) + n + 1)
                for q in range(QN):
                    last = nc.tensor.matmul(
                        img_ps[32 * q:32 * q + 32, 2 * P * (c // 2):2 * P * (c // 2 + 1)],
                        w1[:, k, c % 2, :], xT[:, n % XT, q, :],
                        start=(c % 2 == 0 and k == 0), stop=(c % 2 == 1 and k == KB - 1))
                last.then_inc(projected, 1)

            def sum_moments(loop, turn):
                for c in range(CHUNKS):
                    pe.wait_ge(stats_taken, loop * (TURNS * CHUNKS) + turn * CHUNKS + c + 1)
                    last = nc.tensor.matmul(misc_ps[:, 0:4 * G], ones[:, :],
                                            moments[:, c].rearrange("p m g t -> p (m g t)"),
                                            start=(c == 0), stop=(c == CHUNKS - 1))
                last.then_inc(moments_summed, 1)

            def project_sample(loop, turn, more):
                sum_moments(loop, turn)
                pe.wait_ge(w1_ready, loop * TURNS + turn + 1)
                for step in range(STEPS):
                    ahead = step + LEAD
                    if ahead < STEPS:
                        transpose_step(loop, turn, ahead)
                    elif more:
                        if turn + 1 < TURNS:
                            transpose_step(loop, turn + 1, ahead - STEPS)
                        else:
                            transpose_step(loop + 1, 0, ahead - STEPS)
                    project_step(loop, turn, step)

            for step in range(LEAD):
                transpose_step(0, 0, step)
            project_sample(0, 0, True)
            project_sample(0, 1, True)
            project_sample(0, 2, True)
            with pe.Fori(1, LOOPS) as loop:
                for turn in range(TURNS):
                    project_sample(loop, turn, True)
            project_sample(LOOPS, 0, False)

            pe.wait_ge(xc_copied, B)
            nc.tensor.matmul(misc_ps[0:B, 0:E], pooled[:, :], gate_w[:, :], start=True, stop=True).then_inc(logits_done, 1)
            pe.wait_ge(gate_rows, 1)
            nc.tensor.matmul(misc_ps[:, 64:64 + B * E], ones[0:B, :], gate_diag[:, :, :].rearrange("p b e -> p (b e)"),
                             start=True, stop=True).then_inc(gates_spread, 1)
            pe.wait_ge(w2_replicated, 1)
            for k in range(KB):
                last = nc.tensor.transpose(flat_ps[:, 0, k * P:(k + 1) * P], w2_rep[:, k, :], ident[:, :])
            last.then_inc(w2_transposed, 1)

            def conv_part(order, part):
                for m, ax in part:
                    blk_out, blk_in = blk_ranges(m)
                    col_out, col_in = column_ranges(ax)
                    last = nc.tensor.matmul(
                        img_v[:, blk_out, col_out], band[:, m, ax].rearrange("p h r -> p (h r)"),
                        xc_v[:, order, blk_in, col_in],
                        start=((m, ax) == CONV[0]), stop=((m, ax) == CONV[-1]))
                return last

            def spread_sample(order):
                pe.wait_ge(hi_ready, order + 1)
                pe.wait_ge(lo_ready, order + 1)
                for q in range(QN):
                    if q >= 2:
                        pe.wait_ge(es4_ready, order * QN + q - 1)
                    nc.tensor.matmul(spread_ps[:, q % 2, :], spread[:, q, 0, :], es_hi[:, :], start=True, stop=False)
                    nc.tensor.matmul(spread_ps[:, q % 2, :], spread[:, q, 1, :], es_lo[:, :],
                                     start=False, stop=True).then_inc(spread_done, 1)

            def expand_slot(order, i):
                p, j = slot_place(i)
                for q in range(QN):
                    n = i * QN + q
                    if i == 0:
                        pe.wait_ge(es4_ready, order * QN + q + 1)
                    if not (isinstance(order, int) and order == 0 and n < 2):
                        pe.wait_ge(added, order * TILES + n - 1)
                    for part in (slice(0, 512), slice(512, D)):
                        nc.tensor.matmul(add_ps[:, n % 2, part], all_one[:, :], b2[:, part], start=True, stop=False)
                        last = nc.tensor.matmul(add_ps[:, n % 2, part], es4[:, q, j * P:(j + 1) * P], w2[:, p, part],
                                                start=False, stop=True)
                    last.then_inc(expanded, 1)

            def expand_sample(order, following):
                for i in range(SPS):
                    expand_slot(order, i)
                    if following is not None and 3 <= i < 7:
                        if i == 3:
                            pe.wait_ge(band_ready, order + 2)
                        share = -(-len(CONV) // 4)
                        last = conv_part(following, CONV[(i - 3) * share:(i - 2) * share])
                        if i == 6:
                            last.then_inc(conv_done, 1)

            pe.wait_ge(w2_ready, 1)
            pe.wait_ge(band_ready, 1)
            conv_part(0, CONV).then_inc(conv_done, 1)
            spread_sample(0)
            expand_sample(0, 1)
            with pe.Fori(1, B - 1) as order:
                spread_sample(order)
                expand_sample(order, order + 1)
            spread_sample(B - 1)
            expand_sample(B - 1, None)

        @block.scalar
        def _(act):
            def project_sample(loop, turn):
                for step in range(STEPS):
                    n = turn * STEPS + step
                    act.wait_ge(transposed, loop * (TURNS * STEPS) + n + 1)
                    if not (isinstance(loop, int) and loop == 0 and n < XT):
                        act.wait_ge(projected, loop * (TURNS * STEPS) + n - XT + 1)
                    nc.scalar.copy(xT[:, n % XT], xT_ps[:, n % XT]).then_inc(xT_copied, 1)
                    if step == LEAD - 1:
                        act.wait_ge(variance_ready, loop * TURNS + turn + 1)
                        nc.scalar.activation(norm[:, 1, :], norm[:, 0, :], ACT.Sqrt).then_inc(deviation_ready, 1)
                act.wait_ge(projected, loop * (TURNS * STEPS) + (turn + 1) * STEPS)
                if isinstance(loop, int) and loop == LOOPS:
                    sample, at = B - 1, 0
                else:
                    sample, at = loop * TURNS + turn, loop * TURNS + turn + 1
                nc.scalar.activation(xc[:, at, :], img_ps[:, :], ACT.Identity, bias=bias_1[:, 1:2],
                                     accum_out=pooled[:, bass.ds(sample, 1)] if not isinstance(sample, int)
                                     else pooled[:, sample:sample + 1]).then_inc(xc_copied, 1)

            for turn in range(TURNS):
                project_sample(0, turn)
            with act.Fori(1, LOOPS) as loop:
                for turn in range(TURNS):
                    project_sample(loop, turn)
            project_sample(LOOPS, 0)

            act.wait_ge(logits_max, 1)
            nc.scalar.activation(gate[:, 3, :], gate[:, 0, :], ACT.Exp, bias=gate[:, 2, 0:1]).then_inc(logits_exp, 1)

            def split_sample(order):
                act.wait_ge(conv_done, order + 1)
                nc.scalar.activation(es_hi[:, :], img_ps[:, :], ACT.Identity,
                                     bias=bias_es[:, bass.ds(order, 1)]).then_inc(hi_ready, 1)
                for q in range(QN):
                    act.wait_ge(spread_done, order * QN + q + 1)
                    nc.scalar.copy(es4[:, q, :], spread_ps[:, q % 2, :]).then_inc(es4_ready, 1)

            act.wait_ge(gates_ready, 1)
            with act.Fori(0, B) as order:
                split_sample(order)

        @block.vector
        def _(dve):
            done = [0]
            base = [0]

            def link(ins):
                done[0] += 1
                ins.then_inc(vector_step, 1)
                dve.wait_ge(vector_step, base[0] + done[0])

            dve.wait_ge(consts_ready, 1)
            dve.wait_ge(w1_in_psum, 1)
            nc.vector.tensor_copy(w1T[:, :, :], flat_ps[:, 0, 0:D].rearrange("p (k m) -> p k m", k=KB)[:, :, 0:R])
            link(nc.vector.tensor_reduce(group_sum[:, :], w1_rep.rearrange("p (g c) -> p g c", g=G), AX.X, ALU.add))
            nc.vector.memset(sums[:, :], 0.0).then_inc(weights_ready, 1)

            def expert_taps():
                wl = wl_raw[:, :, :].rearrange("p o (y x) -> p y x o", y=3)
                for e in range(E):
                    for a in range(NT):
                        fresh = True
                        for d in range(3):
                            c = coef[e][d][a]
                            if c == 0.0:
                                continue
                            if fresh:
                                link(nc.vector.tensor_scalar(rows_of[:, a], wl[:, d], c, None, ALU.mult))
                            else:
                                link(nc.vector.scalar_tensor_tensor(rows_of[:, a], wl[:, d], c, rows_of[:, a],
                                                                    ALU.mult, ALU.add))
                            fresh = False
                        if fresh:
                            link(nc.vector.memset(rows_of[:, a], 0.0))
                    for a in range(NT):
                        fresh = True
                        into = experts[:, e, :, a, :]
                        for d in range(3):
                            c = coef[e][d][a]
                            if c == 0.0:
                                continue
                            if fresh:
                                link(nc.vector.tensor_scalar(into, rows_of[:, :, d, :], c, None, ALU.mult))
                            else:
                                link(nc.vector.scalar_tensor_tensor(into, rows_of[:, :, d, :], c, into,
                                                                    ALU.mult, ALU.add))
                            fresh = False
                        if fresh:
                            link(nc.vector.memset(into, 0.0))

            expert_taps()
            nc.vector.memset(bias_1[:, 1:2], 0.0).then_inc(raw_used, 1)
            mean, mean_sq = small[:, 0, :], small[:, 1, :]
            var, dev, inv, tmp = (norm[:, i, :] for i in range(4))
            rs, rs_mean = norm[:, 4, :], norm[:, 5, :]

            def take_stats(loop, turn):
                for c in range(CHUNKS):
                    for s in (2 * c, 2 * c + 1):
                        at = SPS * turn + s
                        dve.wait_ge(loaded[at % SLOTS], loop * 32 + (at // SLOTS + 1) * 16)
                    tiles = chunk((SPS * turn + 2 * c) % SLOTS)
                    for g in range(G):
                        ins = nc.vector.bn_stats(stats[:, c, g, :], tiles[:, :, g * CG:(g + 1) * CG])
                    if c == 0 and not (isinstance(loop, int) and loop == 0 and turn == 0):
                        dve.wait_ge(moments_summed, loop * TURNS + turn)
                    link(ins)
                    by_half = stats[:, c].rearrange("p g (t s) -> p g t s", t=2)
                    nc.vector.tensor_copy(moments[:, c, 0], by_half[:, :, :, 1])
                    link(nc.vector.tensor_tensor(moments[:, c, 1], by_half[:, :, :, 1], by_half[:, :, :, 1], ALU.mult))
                    nc.vector.scalar_tensor_tensor(moments[:, c, 1], by_half[:, :, :, 2], 1.0 / (2 * QN * CG // 2),
                                                   moments[:, c, 1], ALU.mult, ALU.add).then_inc(stats_taken, 1)

            def fold_norm(loop, turn):
                dve.wait_ge(moments_summed, loop * TURNS + turn + 1)
                link(nc.vector.tensor_reduce(small[:, :, :], misc_ps[:, 0:4 * G].rearrange("p (m g t) -> p m g t", m=2, t=2),
                                             AX.X, ALU.add))
                link(nc.vector.tensor_tensor(tmp, mean, mean, ALU.mult))
                link(nc.vector.tensor_tensor(var, mean_sq, tmp, ALU.subtract))
                nc.vector.tensor_scalar(var, var, 0.0, GN_EPS, ALU.max, ALU.add).then_inc(variance_ready, 1)
                dve.wait_ge(deviation_ready, loop * TURNS + turn + 1)
                link(nc.vector.reciprocal(inv, dev))
                link(nc.vector.tensor_tensor(tmp, inv, inv, ALU.mult))
                link(nc.vector.tensor_tensor(tmp, tmp, var, ALU.mult))
                link(nc.vector.tensor_scalar(tmp, tmp, -0.5, 1.5, ALU.mult, ALU.add))
                link(nc.vector.tensor_tensor(rs, inv, tmp, ALU.mult))
                link(nc.vector.tensor_tensor(rs_mean, rs, mean, ALU.mult))
                link(nc.vector.tensor_tensor(picked[:, :, :], rs.unsqueeze(1).broadcast_to([P, KB, G]), group_of[:, :, :], ALU.mult))
                link(nc.vector.tensor_reduce(of_channel[:, :], picked[:, :, :], AX.X, ALU.add))
                if not (isinstance(loop, int) and loop == 0 and turn == 0):
                    dve.wait_ge(xc_copied, loop * TURNS + turn)
                link(nc.vector.scalar_tensor_tensor(tmp, rs_mean, 1.0, group_sum[:, :], ALU.mult, ALU.mult,
                                                    accum_out=sums[:, 0:1]))
                link(nc.vector.tensor_tensor(bias_1[:, 1:2], bias_1[:, 0:1], sums[:, 0:1], ALU.subtract))
                for p in range(2):
                    ins = nc.vector.tensor_tensor(w1[:, :, p, p * R:(p + 1) * R], w1T[:, :, :],
                                                  of_channel[:, :].unsqueeze(2).broadcast_to([P, KB, R]), ALU.mult)
                ins.then_inc(w1_ready, 1)

            for turn in range(TURNS):
                take_stats(0, turn)
                fold_norm(0, turn)
            start = done[0]
            LINKS = TURNS * (2 * CHUNKS + 13)
            with dve.Fori(1, LOOPS) as loop:
                base[0] = (loop - 1) * LINKS
                for turn in range(TURNS):
                    take_stats(loop, turn)
                    fold_norm(loop, turn)
            assert done[0] - start == LINKS, done[0] - start
            base[0] = (LOOPS - 2) * LINKS
            take_stats(LOOPS, 0)
            fold_norm(LOOPS, 0)

            logits, rank, neg_max, expo, gate_of = gate[:, 0, :], gate[:, 1, :], gate[:, 2, 0:1], gate[:, 3, :], gate[:, 4, :]
            dve.wait_ge(logits_done, 1)
            link(nc.vector.scalar_tensor_tensor(logits, misc_ps[0:B, 0:E], 1.0 / (HH * WW), gate_b[:, :], ALU.mult, ALU.add))
            link(nc.vector.tensor_reduce(neg_max, logits, AX.X, ALU.max, negate=True))
            nc.vector.memset(rank, 0.0).then_inc(logits_max, 1)
            for j in range(E):
                dve.wait_ge(logits_max, 1)
                link(nc.vector.scalar_tensor_tensor(rank, logits, logits[:, j:j + 1], rank, ALU.is_lt, ALU.add))
                if j + 1 < E:
                    link(nc.vector.scalar_tensor_tensor(rank[:, j + 1:E], logits[:, j + 1:E], logits[:, j:j + 1],
                                                        rank[:, j + 1:E], ALU.is_equal, ALU.add))
            link(nc.vector.tensor_scalar(rank, rank, 1.5, None, ALU.is_lt))
            dve.wait_ge(logits_exp, 1)
            link(nc.vector.tensor_tensor(expo, expo, rank, ALU.mult))
            link(nc.vector.tensor_reduce(gate[:, 5, 0:1], expo, AX.X, ALU.add))
            link(nc.vector.reciprocal(gate[:, 6, 0:1], gate[:, 5, 0:1]))
            link(nc.vector.tensor_scalar(gate_of, expo, gate[:, 6, 0:1], None, ALU.mult))
            nc.vector.tensor_tensor(gate_diag[:, :, :], gate_of.unsqueeze(1).broadcast_to([B, B, E]),
                                    ident[0:B, 0:B].unsqueeze(2).broadcast_to([B, B, E]), ALU.mult).then_inc(gate_rows, 1)
            dve.wait_ge(gates_spread, 1)
            table = misc_ps[:, 64:64 + B * E].rearrange("p (e b) -> p b e", e=E)
            whole = float(P * CHUNKS * 2)
            nc.vector.tensor_scalar(gates[:, 0, :], table[:, B - 1, :], whole, None, ALU.mult)
            link(nc.vector.tensor_scalar(gates[:, 1:B, :], table[:, 0:B - 1, :], whole, None, ALU.mult))
            link(nc.vector.tensor_reduce(bias_es[:, :], gates[:, :, :], AX.X, ALU.add))
            link(nc.vector.tensor_scalar(bias_es[:, :], bias_es[:, :], bias_l[:, 0:1], None, ALU.mult))
            nc.vector.memset(small[:, 0, 0:1], 0.0).then_inc(gates_ready, 1)
            nc.vector.memset(small[:, 0, 1:2], 0.0).then_inc(high_free, 1)
            dve.wait_ge(w2_in, 3 * 16)
            full = [P, KB, NH, R]
            nc.vector.tensor_copy(w2_rep[:, :, :].rearrange("p k (n r) -> p k n r", n=NH),
                                  w2_raw[:, :, :].unsqueeze(2).broadcast_to(full)).then_inc(w2_replicated, 1)
            for p in range(2):
                for part in range(2):
                    link(nc.vector.tensor_tensor(row_kind[:, 2 * p + part:2 * p + part + 1],
                                                 masks[:, SAME, 2 * part + p, 0:1], masks[:, SAME, 4 + 2 * part + p, 0:1], ALU.add))
            nc.vector.memset(all_one[:, :].bitcast(F32), 1.0)
            link(nc.vector.memset(spread[:, :, :, :].bitcast(F32), 0.0))
            for q in range(QN):
                own = ident[:, 2 * R * q:2 * R * (q + 1)]
                for part in range(4):
                    nc.vector.tensor_copy(spread[:, q, part // 2, 2 * R * part:2 * R * (part + 1)], own)
            dve.wait_ge(w2_transposed, 1)
            link(nc.vector.tensor_copy(w2_hi[:, :], flat_ps[:, 0, 0:D]))
            link(nc.vector.tensor_tensor(w2_lo[:, :], flat_ps[:, 0, 0:D], w2_hi[:, :].bitcast(F32), ALU.subtract))
            w2_part = w2_rep[:, :, :].rearrange("p k m -> p (k m)")
            for p in range(2):
                link(nc.vector.tensor_scalar(w2_part, w2_lo[:, :], row_kind[:, 2 * p + 1:2 * p + 2], None, ALU.mult))
                link(nc.vector.scalar_tensor_tensor(w2[:, p, :], w2_hi[:, :].bitcast(F32), row_kind[:, 2 * p:2 * p + 1],
                                                    w2_part, ALU.mult, ALU.add))
            link(nc.vector.tensor_copy(b2[:, :], b2_raw[:, :]))
            nc.vector.tensor_tensor(b2[32:64, :], b2_raw[32:64, :], b2[32:64, :].bitcast(F32),
                                    ALU.subtract).then_inc(w2_ready, 1)

            def gated_taps(order):
                for e in range(E):
                    g = gates[:, order, e:e + 1]
                    flat = "p a x r -> p (a x r)"
                    of_e, all_e = experts[:, e].rearrange(flat), taps[:, :, :, :].rearrange(flat)
                    if e == 0:
                        ins = nc.vector.tensor_scalar(all_e, of_e, g, None, ALU.mult)
                    else:
                        ins = nc.vector.scalar_tensor_tensor(all_e, of_e, g, all_e, ALU.mult, ALU.add)
                    if e < E - 1:
                        link(ins)
                ins.then_inc(taps_ready, 1)

            def low_half(order):
                dve.wait_ge(hi_ready, order + 1)
                nc.vector.scalar_tensor_tensor(es_lo[:, :], img_ps[:, :], bias_es[:, bass.ds(order, 1)],
                                               es_hi[:, :].bitcast(F32), ALU.add, ALU.subtract).then_inc(lo_ready, 1)

            def add_sample(order, more):
                if more:
                    dve.wait_ge(band_ready, order + 1)
                    gated_taps(order + 1)
                for i in range(SPS):
                    if more and i == SPS - 1:
                        low_half(order + 1)
                    uses = -(-(B * SPS - i) // SLOTS)
                    dve.wait_ge(loaded[i], (order + uses) * 16)
                    for q in range(QN):
                        n = i * QN + q
                        dve.wait_ge(expanded, order * TILES + n + 1)
                        nc.vector.tensor_tensor(slot(i)[:, q, :], slot(i)[:, q, :], add_ps[:, n % 2, :],
                                                ALU.add).then_inc(added, 1)

            gated_taps(0)
            low_half(0)
            start, before = done[0], base[0]
            with dve.Fori(0, B - 1) as order:
                base[0] = before + order * (E - 1)
                add_sample(order, True)
            assert done[0] - start == E - 1
            base[0] = before + (B - 2) * (E - 1)
            add_sample(B - 1, False)


_INPUTS = ["x", "L0_conv_conv1_w", "L0_conv_conv1_b", "L0_conv_convl_w", "L0_conv_convl_b",
           "L0_conv_conv2_w", "L0_conv_conv2_b", "L0_conv_H_w", "L0_conv_H_b"]


def kernel(**inputs):
    import numpy as np
    import concourse.bacc as bacc
    from concourse import mybir as mb
    from concourse.bass_utils import run_bass_kernel_spmd

    nc = bacc.Bacc("TRN2", target_bir_lowering=False, num_devices=1)
    arrays, args = {}, []
    for name in _INPUTS:
        a = np.ascontiguousarray(inputs[name])
        arrays[f"in_{name}"] = a
        args.append(nc.dram_tensor(f"in_{name}", a.shape, mb.dt.from_np(a.dtype), kind="ExternalInput").ap())
    args.append(nc.dram_tensor("out", (B, HH, WW, D), F32, kind="ExternalOutput").ap())
    program(nc, *args)
    result = run_bass_kernel_spmd(nc, [arrays], core_ids=[0])
    return result.results[0]["out"]
```

```python
from contextlib import ExitStack

import concourse.bass as bass
from concourse import mybir

F32 = mybir.dt.float32
F32R = mybir.dt.float32r
ALU = mybir.AluOpType
ACT = mybir.ActivationFunctionType
AX = mybir.AxisListType

P = 128
B, HH, WW, D = 16, 64, 64, 768
R, E = 16, 4
G = 32
CG = D // G
KB = D // P
NH = P // R
NB = HH // NH
PIX = NB * WW
QN = 4
TILES = HH * WW // P
SPS = TILES // QN
CHUNKS = SPS // 2
SLOTS = 12
LOW = 8
TURNS = 3
LOOPS = (B - 1) // TURNS
STEPS = CHUNKS * KB
XT_PS = 3
XT = 6
LEAD = KB
BATCHES = [4, 2, 2]
SUM_AT = 22
MOMENT_OPS = 2
FOLD_OPS = 13
GN_EPS = 1e-5
LEFT, MID, RIGHT, LEFT_EDGE, RIGHT_EDGE = range(5)
NT = 5
UP, HERE, DOWN, FROM_ABOVE, FROM_BELOW, TOP, BOTTOM = range(7)
MAT_ROW_TAP = [LEFT, MID, RIGHT, LEFT, RIGHT, LEFT_EDGE, RIGHT_EDGE]
SAME, ABOVE, BELOW, FIRST, LAST = range(5)
MAT_MASK = [SAME, SAME, SAME, ABOVE, BELOW, FIRST, LAST]


def resize_taps():
    coef = []
    for e in range(E):
        f = 2 ** e
        sampled = [0] if f == 1 else [f // 2 - 1, f // 2]
        of_expert = []
        for d in (-1, 0, 1):
            inner = {-1: 0.0, 0: 0.0, 1: 0.0}
            first = last = 0.0
            for k in sampled:
                at = (k + d + 0.5) / f - 0.5
                low = int(at // 1)
                for offset, part in ((low, 1 - (at - low)), (low + 1, at - low)):
                    part /= len(sampled)
                    if not part:
                        continue
                    inner[offset] += part
                    if k + d >= 0 and offset <= 0:
                        first += part
                    if k + d < f and offset >= 0:
                        last += part
            of_expert.append([inner[-1], inner[0], inner[1], first - inner[0], last - inner[0]])
        coef.append(of_expert)
    return coef


def slot_place(i):
    return (i // 2) % 2, 2 * (i // 4) + i % 2


def column_ranges(ax):
    return {LEFT: (slice(1, WW), slice(0, WW - 1)), MID: (slice(0, WW), slice(0, WW)),
            RIGHT: (slice(0, WW - 1), slice(1, WW)), LEFT_EDGE: (slice(0, 1), slice(0, 1)),
            RIGHT_EDGE: (slice(WW - 1, WW), slice(WW - 1, WW))}[ax]


def blk_ranges(m):
    return {UP: (slice(1, NB), slice(0, NB - 1)), HERE: (slice(0, NB), slice(0, NB)),
            DOWN: (slice(0, NB - 1), slice(1, NB)), FROM_ABOVE: (slice(0, 1), slice(NB - 1, NB)),
            FROM_BELOW: (slice(NB - 1, NB), slice(0, 1)), TOP: (slice(0, 1), slice(0, 1)),
            BOTTOM: (slice(NB - 1, NB), slice(NB - 1, NB))}[m]


MAT_ORDER = [HERE, UP, DOWN, FROM_ABOVE, FROM_BELOW, TOP, BOTTOM]
CONV = [(m, a) for m in MAT_ORDER for a in (MID, LEFT, RIGHT, LEFT_EDGE, RIGHT_EDGE)]


def program(nc, x, conv1_w, conv1_b, convl_w, convl_b, conv2_w, conv2_b, H_w, H_b, out):
    slots_of = "b (q p j bb) w c -> b p j (bb w) q c"
    x_v = x.rearrange(slots_of, q=QN, p=2, j=4, bb=2)
    out_v = out.rearrange(slots_of, q=QN, p=2, j=4, bb=2)
    coef = resize_taps()

    ctx = ExitStack()
    scratch = ExitStack()
    with ctx:
        def sb(name, shape, dt=F32, stack=ctx):
            return stack.enter_context(nc.sbuf_tensor(name, shape, dt))

        def sem(name):
            return ctx.enter_context(nc.semaphore(name))

        x_low = sb("x_low", [P, LOW, QN, D])
        xc = sb("xc", [P, B, PIX])
        ident = sb("ident", [P, P])
        pooled = sb("pooled", [P, B])
        small = sb("small", [P, 2, G])
        x_high = sb("x_high", [P, SLOTS - LOW, QN, D], stack=scratch)
        xT = sb("xT", [P, XT, QN, 2 * P], stack=scratch)
        w1T = sb("w1T", [P, KB, R], stack=scratch)
        w1_first = sb("w1_first", [P, KB, 2, 2 * R], stack=scratch)
        group_sum = sb("group_sum", [P, G], stack=scratch)
        group_of = sb("group_of", [P, KB, G], stack=scratch)
        stats = sb("stats", [P, G, 6], stack=scratch)
        moments = sb("moments", [P, len(BATCHES), 2, G, 2], stack=scratch)
        ones = sb("ones", [P, P], stack=scratch)
        norm = sb("norm", [P, 6, G], stack=scratch)
        of_channel = sb("of_channel", [P, KB], stack=scratch)
        bias_1 = sb("bias_1", [P, 1 + TURNS], stack=scratch)
        sums = sb("sums", [P, 2], stack=scratch)
        picked = stats[:, :, :].rearrange("p g t -> p (g t)").rearrange("p (k g) -> p k g", k=KB)
        w1 = [w1_first] + [xc[:, at, 0:KB * 4 * R].rearrange("p (k n r) -> p k n r", k=KB, n=2) for at in (B - 1, 0)]
        w1_rep = x_high[:, SLOTS - LOW - 1, 0, :]
        gate = xT[0:B, 0, 0, 0:8 * E].rearrange("b (i e) -> b i e", i=8)
        gate_diag = xT[0:B, 1, 0, 0:B * E].rearrange("b (s e) -> b s e", s=B)
        scratch.close()
        masks = sb("masks", [P, 5, NH, R])
        experts = sb("experts", [P, E, NT, NT, R])
        gates = sb("gates", [P, B, E])
        bias_l = sb("bias_l", [P, 1])
        bias_es = sb("bias_es", [P, B])
        gate_w = sb("gate_w", [P, E])
        gate_b = sb("gate_b", [R, E])
        wl_raw = sb("wl_raw", [P, R, 9])
        rows_of = sb("rows_of", [P, NT, 3, R])
        spread = sb("spread", [P, QN, 2, P], F32R)
        w2 = sb("w2", [P, 2, D], F32R)
        b2 = sb("b2", [P, D], F32R)
        all_one = sb("all_one", [P, P], F32R)
        w2_raw = sb("w2_raw", [P, KB, R])
        row_kind = sb("row_kind", [P, 4])
        w2_rep = sb("w2_rep", [P, KB, P])
        w2_hi = sb("w2_hi", [P, D], F32R)
        w2_lo = sb("w2_lo", [P, D])
        b2_raw = sb("b2_raw", [P, D])
        taps = sb("taps", [P, NT, NT, R])
        es_hi = sb("es_hi", [P, PIX], F32R)
        es_lo = sb("es_lo", [P, PIX], F32R)
        band = sb("band", [P, 7, NT, NH, R])
        es4 = sb("es4", [P, QN, PIX], F32R)

        xT_ps = ctx.enter_context(nc.psum_tensor("xT_ps", [P, XT_PS, QN, 2 * P], F32))
        img_ps = ctx.enter_context(nc.psum_tensor("img_ps", [P, PIX], F32))
        misc_ps = ctx.enter_context(nc.psum_tensor("misc_ps", [P, 512], F32))
        flat_ps = xT_ps[:, :, :, :].rearrange("p n q c -> p n (q c)")
        add_ps = flat_ps[:, 0:2, 0:D]
        spread_ps = flat_ps[:, 2, :].rearrange("p (n c) -> p n c", n=2)
        w1_ps = [(img_ps if k < 4 else misc_ps)[:, k % 4 * P:(k % 4 + 1) * P] for k in range(KB)]
        img_v = img_ps[:, :].rearrange("p (k w) -> p k w", w=WW)
        xc_v = xc[:, :, :].rearrange("p b (k w) -> p b k w", w=WW)

        def slot(n):
            return x_low[:, n] if n < LOW else x_high[:, n - LOW]

        def tiles_of(n, count):
            part = x_low[:, n:n + count] if n < LOW else x_high[:, n - LOW:n - LOW + count]
            return part.rearrange("p s q c -> p (s q) c")

        loaded = [sem(f"loaded{n}") for n in range(SLOTS)]
        weights_in = sem("weights_in")
        consts_ready = sem("consts_ready")
        w1_laid_out = sem("w1_laid_out")
        w1_in_psum = sem("w1_in_psum")
        stats_taken = sem("stats_taken")
        transposed = sem("transposed")
        xT_copied = sem("xT_copied")
        projected = sem("projected")
        moments_summed = sem("moments_summed")
        variance_ready = sem("variance_ready")
        deviation_ready = sem("deviation_ready")
        w1_ready = sem("w1_ready")
        xc_copied = sem("xc_copied")
        vector_step = sem("vector_step")
        pool_step = sem("pool_step")
        logits_done = sem("logits_done")
        logits_max = sem("logits_max")
        logits_exp = sem("logits_exp")
        gates_spread = sem("gates_spread")
        gate_rows = sem("gate_rows")
        masks_ready = sem("masks_ready")
        bias_zero = sem("bias_zero")
        wl_in = sem("wl_in")
        late_weights_in = sem("late_weights_in")
        gates_ready = sem("gates_ready")
        w2_replicated = sem("w2_replicated")
        w2_transposed = sem("w2_transposed")
        w2_ready = sem("w2_ready")
        high_free = sem("high_free")
        band_ready = sem("band_ready")
        conv_done = sem("conv_done")
        hi_ready = sem("hi_ready")
        lo_ready = sem("lo_ready")
        spread_done = sem("spread_done")
        es4_ready = sem("es4_ready")
        expanded = sem("expanded")
        added = sem("added")
        stored = [sem(f"stored{n}") for n in range(LOW)]

        block = ctx.enter_context(nc.Block())

        @block.sync
        def _(sp):
            def load(sample, i, n):
                p, j = slot_place(i)
                sp.dma_start(slot(n), x_v[sample, p, j]).then_inc(loaded[n], 16)

            def load_sample(loop, turn, first):
                for i in range(SPS):
                    at = SPS * turn + i
                    if not (first and at < SLOTS):
                        if i % 2 == 0:
                            last = (at - SLOTS) // 2 + 1
                            sp.wait_ge(transposed, loop * (TURNS * STEPS) + last * KB)
                    if first and at == BATCHES[0]:
                        load_weights()
                    if first and at == SLOTS - 1:
                        sp.wait_ge(w1_laid_out, 1)
                    load(loop * TURNS + turn, i, at % SLOTS)

            def load_weights():
                for h in range(NH):
                    rows = slice(R * h, R * h + R)
                    sp.dma_start(w1_rep[rows, :], conv1_w.rearrange("r c y x -> r (c y x)")).then_inc(weights_in, 16)
                    sp.dma_start(bias_1[rows, 0:1], conv1_b.unsqueeze(1)).then_inc(weights_in, 16)

            def load_late_weights():
                sp.wait_ge(high_free, 1)
                for h in range(NH):
                    sp.dma_start(wl_raw[R * h:R * h + R, :, :], convl_w.rearrange("o i y x -> i o (y x)")
                                 ).then_inc(wl_in, 16)
                sp.wait_ge(bias_zero, 1)
                for row in (0, 32):
                    sp.dma_start(b2_raw[row:row + 1, :], conv2_b.unsqueeze(0)).then_inc(late_weights_in, 16)
                sp.dma_start(w2_raw[:, :, :], conv2_w.rearrange("(k c) r y x -> c k (r y x)", k=KB)
                             ).then_inc(late_weights_in, 16)
                sp.dma_start(gate_b[:, :], H_b.partition_broadcast(R)).then_inc(late_weights_in, 16)
                for h in range(NH):
                    rows = slice(R * h, R * h + R)
                    sp.dma_start(bias_l[rows, :], convl_b.unsqueeze(1)).then_inc(late_weights_in, 16)
                    sp.dma_start(gate_w[rows, :], H_w.rearrange("e r -> r e"),
                                 allow_slow_non_contiguous=True).then_inc(late_weights_in, 16)

            for turn in range(TURNS):
                load_sample(0, turn, True)
            with sp.Fori(1, LOOPS) as loop:
                for turn in range(TURNS):
                    load_sample(loop, turn, False)
            load_sample(LOOPS, 0, False)
            load_late_weights()

            def store(order, sample, i):
                p, j = slot_place(i)
                sp.wait_ge(added, order * TILES + (i + 1) * QN)
                sp.dma_start(out_v[sample, p, j], slot(i)).then_inc(stored[i], 16)

            def reload(order, sample, i):
                sp.wait_ge(stored[i], order * 16 + 16)
                load(sample, i, i)

            def store_and_reload(order, sample, following):
                for i in range(SPS):
                    store(order, sample, i)
                    if i >= 2:
                        reload(order, following, i - 2)
                for i in (SPS - 2, SPS - 1):
                    reload(order, following, i)

            store_and_reload(0, B - 1, 0)
            with sp.Fori(1, B - 1) as order:
                store_and_reload(order, order - 1, order)
            for i in range(SPS):
                store(B - 1, B - 2, i)
            for i in range(SPS):
                sp.wait_ge(stored[i], 16 * B)

        @block.gpsimd
        def _(pool):
            done = [0]

            def link(ins):
                done[0] += 1
                ins.then_inc(pool_step, 1)
                pool.wait_ge(pool_step, done[0])

            def keep_where(tile, base, pattern, per_partition):
                link(nc.gpsimd.affine_select(out=tile, in_=tile, compare_op=ALU.is_ge, fill=0.0, base=base,
                                             pattern=pattern, channel_multiplier=per_partition))

            link(nc.gpsimd.memset(ident[:, :], 0.0))
            link(nc.gpsimd.affine_select(out=ident[:, :], in_=ident[:, :], compare_op=ALU.not_equal, fill=1.0,
                                         base=0, pattern=[[-1, P]], channel_multiplier=1))
            link(nc.gpsimd.memset(group_of[:, :, :], 1.0))
            keep_where(group_of[:, :, :], 0, [[P, KB], [-CG, G]], 1)
            keep_where(group_of[:, :, :], CG - 1, [[-P, KB], [CG, G]], -1)
            link(nc.gpsimd.memset(ones[:, :], 1.0 / (P * SPS * 2)))
            for turn in range(TURNS):
                ins = nc.gpsimd.memset(w1[turn][:, :, :, :], 0.0)
            ins.then_inc(consts_ready, 1)

            pool.wait_ge(high_free, 1)
            nc.gpsimd.memset(b2_raw[:, :], 0.0).then_inc(bias_zero, 1)
            link(nc.gpsimd.memset(masks[:, :, :, :], 1.0))
            for kind, shift in ((SAME, 0), (ABOVE, -1), (BELOW, 1), (FIRST, 0), (LAST, 0)):
                keep_where(masks[:, kind], -R * shift, [[-R, NH], [0, R]], 1)
                keep_where(masks[:, kind], R * shift + R - 1, [[R, NH], [0, R]], -1)
            link(nc.gpsimd.memset(masks[:, FIRST, 1:NH], 0.0))
            nc.gpsimd.memset(masks[:, LAST, 0:NH - 1], 0.0).then_inc(masks_ready, 1)

        @block.tensor
        def _(pe):
            pe.wait_ge(consts_ready, 1)
            def transpose_step(loop, turn, step):
                c, k = divmod(step, KB)
                n = turn * STEPS + step
                buf = n % XT_PS
                if k == 0:
                    for s in (2 * c, 2 * c + 1):
                        at = SPS * turn + s
                        pe.wait_ge(loaded[at % SLOTS], loop * 32 + (at // SLOTS + 1) * 16)
                if not (isinstance(loop, int) and loop == 0 and n < XT_PS):
                    pe.wait_ge(xT_copied, loop * (TURNS * STEPS) + n - XT_PS + 1)
                if step == KB - 1:
                    pe.wait_ge(stats_taken, (loop * TURNS + turn) * len(BATCHES) + 1)
                for q in range(QN):
                    for half in range(2):
                        last = nc.tensor.transpose(
                            xT_ps[:, buf, q, half * P:(half + 1) * P],
                            slot((SPS * turn + 2 * c + half) % SLOTS)[:, q, k * P:(k + 1) * P], ident[:, :])
                last.then_inc(transposed, 1)

            def project_step(loop, turn, step):
                c, k = divmod(step, KB)
                n = turn * STEPS + step
                pe.wait_ge(xT_copied, loop * (TURNS * STEPS) + n + 1)
                for q in range(QN):
                    last = nc.tensor.matmul(
                        img_ps[32 * q:32 * q + 32, 2 * P * (c // 2):2 * P * (c // 2 + 1)],
                        w1[turn][:, k, c % 2, :], xT[:, n % XT, q, :],
                        start=(c % 2 == 0 and k == 0), stop=(c % 2 == 1 and k == KB - 1))
                last.then_inc(projected, 1)

            def sum_moments(loop, turn):
                count = len(BATCHES)
                for i in range(count):
                    pe.wait_ge(stats_taken, loop * (TURNS * count) + turn * count + i + 1)
                    last = nc.tensor.matmul(misc_ps[:, 0:4 * G], ones[:, :],
                                            moments[:, i].rearrange("p m g t -> p (m g t)"),
                                            start=(i == 0), stop=(i == count - 1))
                last.then_inc(moments_summed, 1)

            def project_sample(loop, turn, more):
                following = (loop, turn + 1) if turn + 1 < TURNS else (loop + 1, 0)
                pe.wait_ge(w1_ready, loop * TURNS + turn + 1)
                for step in range(STEPS):
                    if step + LEAD < STEPS:
                        transpose_step(loop, turn, step + LEAD)
                    elif more:
                        transpose_step(*following, step + LEAD - STEPS)
                    if step == 0 and not (isinstance(loop, int) and loop == 0 and turn == 0):
                        pe.wait_ge(xc_copied, loop * TURNS + turn)
                    project_step(loop, turn, step)
                    if step == SUM_AT and more:
                        sum_moments(*following)

            for step in range(LEAD):
                transpose_step(0, 0, step)
            pe.wait_ge(weights_in, 2 * NH * 16)
            for k in range(KB):
                last = nc.tensor.transpose(w1_ps[k], w1_rep[:, k * P:(k + 1) * P], ident[:, :])
            last.then_inc(w1_in_psum, 1)
            pe.wait_ge(w1_laid_out, 1)
            sum_moments(0, 0)
            for turn in range(TURNS):
                project_sample(0, turn, True)
            with pe.Fori(1, LOOPS) as loop:
                for turn in range(TURNS):
                    project_sample(loop, turn, True)
            project_sample(LOOPS, 0, False)

            pe.wait_ge(w2_replicated, 1)
            pe.wait_ge(xc_copied, B)
            for k in range(KB):
                last = nc.tensor.transpose(flat_ps[:, 0, k * P:(k + 1) * P], w2_rep[:, k, :], ident[:, :])
            last.then_inc(w2_transposed, 1)
            nc.tensor.matmul(misc_ps[0:B, 0:E], pooled[:, :], gate_w[:, :], start=True, stop=True).then_inc(logits_done, 1)
            pe.wait_ge(gate_rows, 1)
            nc.tensor.matmul(misc_ps[:, 64:64 + B * E], ones[0:B, :], gate_diag[:, :, :].rearrange("p b e -> p (b e)"),
                             start=True, stop=True).then_inc(gates_spread, 1)
            def conv_part(order, part):
                for m, ax in part:
                    if ax == MID:
                        pe.wait_ge(band_ready, order * 7 + MAT_ORDER.index(m) + 1)
                    blk_out, blk_in = blk_ranges(m)
                    col_out, col_in = column_ranges(ax)
                    last = nc.tensor.matmul(
                        img_v[:, blk_out, col_out], band[:, m, ax].rearrange("p h r -> p (h r)"),
                        xc_v[:, order, blk_in, col_in],
                        start=((m, ax) == CONV[0]), stop=((m, ax) == CONV[-1]))
                return last

            def spread_sample(order):
                pe.wait_ge(hi_ready, order + 1)
                pe.wait_ge(lo_ready, order + 1)
                for q in range(QN):
                    if q >= 2:
                        pe.wait_ge(es4_ready, order * QN + q - 1)
                    nc.tensor.matmul(spread_ps[:, q % 2, :], spread[:, q, 0, :], es_hi[:, :], start=True, stop=False)
                    nc.tensor.matmul(spread_ps[:, q % 2, :], spread[:, q, 1, :], es_lo[:, :],
                                     start=False, stop=True).then_inc(spread_done, 1)

            def expand_slot(order, i):
                p, j = slot_place(i)
                for q in range(QN):
                    n = i * QN + q
                    if i == 0:
                        pe.wait_ge(es4_ready, order * QN + q + 1)
                    if not (isinstance(order, int) and order == 0 and n < 2):
                        pe.wait_ge(added, order * TILES + n - 1)
                    for part in (slice(0, 512), slice(512, D)):
                        nc.tensor.matmul(add_ps[:, n % 2, part], all_one[:, :], b2[:, part], start=True, stop=False)
                        last = nc.tensor.matmul(add_ps[:, n % 2, part], es4[:, q, j * P:(j + 1) * P], w2[:, p, part],
                                                start=False, stop=True)
                    last.then_inc(expanded, 1)

            def expand_sample(order, following):
                for i in range(SPS):
                    expand_slot(order, i)
                    if following is not None and 3 <= i < 7:
                        share = -(-len(CONV) // 4)
                        last = conv_part(following, CONV[(i - 3) * share:(i - 2) * share])
                        if i == 6:
                            last.then_inc(conv_done, 1)

            conv_part(0, CONV).then_inc(conv_done, 1)
            pe.wait_ge(w2_ready, 1)
            spread_sample(0)
            expand_sample(0, 1)
            with pe.Fori(1, B - 1) as order:
                spread_sample(order)
                expand_sample(order, order + 1)
            spread_sample(B - 1)
            expand_sample(B - 1, None)

        @block.scalar
        def _(act):
            def copy_step(loop, turn, step):
                n = turn * STEPS + step
                act.wait_ge(transposed, loop * (TURNS * STEPS) + n + 1)
                if not (isinstance(loop, int) and loop == 0 and n < XT):
                    act.wait_ge(projected, loop * (TURNS * STEPS) + n - XT + 1)
                nc.scalar.copy(xT[:, n % XT], xT_ps[:, n % XT_PS]).then_inc(xT_copied, 1)

            def deviation(loop, turn):
                act.wait_ge(variance_ready, loop * TURNS + turn + 1)
                nc.scalar.activation(norm[:, 1, :], norm[:, 0, :], ACT.Sqrt).then_inc(deviation_ready, 1)

            def copy_image(loop, turn, sample, at):
                act.wait_ge(projected, loop * (TURNS * STEPS) + (turn + 1) * STEPS)
                nc.scalar.activation(xc[:, at, :], img_ps[:, :], ACT.Identity, bias=bias_1[:, 1 + turn:2 + turn],
                                     accum_out=pooled[:, bass.ds(sample, 1)]).then_inc(xc_copied, 1)

            def copy_sample(loop, turn):
                for step in range(LEAD, STEPS):
                    copy_step(loop, turn, step)
                following = (loop, turn + 1) if turn + 1 < TURNS else (loop + 1, 0)
                for step in range(LEAD):
                    copy_step(*following, step)
                    if step == SUM_AT + LEAD - STEPS:
                        deviation(*following)
                copy_image(loop, turn, loop * TURNS + turn, loop * TURNS + turn + 1)

            for step in range(LEAD):
                copy_step(0, 0, step)
            deviation(0, 0)
            for turn in range(TURNS):
                copy_sample(0, turn)
            with act.Fori(1, LOOPS) as loop:
                for turn in range(TURNS):
                    copy_sample(loop, turn)
            for step in range(LEAD, STEPS):
                copy_step(LOOPS, 0, step)
            copy_image(LOOPS, 0, B - 1, 0)

            act.wait_ge(logits_max, 1)
            nc.scalar.activation(gate[:, 3, :], gate[:, 0, :], ACT.Exp, bias=gate[:, 2, 0:1]).then_inc(logits_exp, 1)

            def split_sample(order):
                act.wait_ge(conv_done, order + 1)
                nc.scalar.activation(es_hi[:, :], img_ps[:, :], ACT.Identity,
                                     bias=bias_es[:, bass.ds(order, 1)]).then_inc(hi_ready, 1)
                for q in range(QN):
                    act.wait_ge(spread_done, order * QN + q + 1)
                    nc.scalar.copy(es4[:, q, :], spread_ps[:, q % 2, :]).then_inc(es4_ready, 1)

            act.wait_ge(gates_ready, 1)
            with act.Fori(0, B) as order:
                split_sample(order)

        @block.vector
        def _(dve):
            done = [0]
            base = [0]

            def link(ins):
                done[0] += 1
                ins.then_inc(vector_step, 1)
                dve.wait_ge(vector_step, base[0] + done[0])

            dve.wait_ge(consts_ready, 1)

            def lay_out_w1():
                dve.wait_ge(w1_in_psum, 1)
                for k in range(KB):
                    nc.vector.tensor_copy(w1T[:, k, :], w1_ps[k][:, 0:R])
                nc.vector.tensor_reduce(group_sum[:, :], w1_rep.rearrange("p (g c) -> p g c", g=G), AX.X,
                                        ALU.add).then_inc(w1_laid_out, 1)

            def expert_taps():
                wl = wl_raw[:, :, :].rearrange("p o (y x) -> p y x o", y=3)
                for e in range(E):
                    for a in range(NT):
                        fresh = True
                        for d in range(3):
                            c = coef[e][d][a]
                            if c == 0.0:
                                continue
                            if fresh:
                                link(nc.vector.tensor_scalar(rows_of[:, a], wl[:, d], c, None, ALU.mult))
                            else:
                                link(nc.vector.scalar_tensor_tensor(rows_of[:, a], wl[:, d], c, rows_of[:, a],
                                                                    ALU.mult, ALU.add))
                            fresh = False
                        if fresh:
                            link(nc.vector.memset(rows_of[:, a], 0.0))
                    for a in range(NT):
                        fresh = True
                        into = experts[:, e, :, a, :]
                        for d in range(3):
                            c = coef[e][d][a]
                            if c == 0.0:
                                continue
                            if fresh:
                                link(nc.vector.tensor_scalar(into, rows_of[:, :, d, :], c, None, ALU.mult))
                            else:
                                link(nc.vector.scalar_tensor_tensor(into, rows_of[:, :, d, :], c, into,
                                                                    ALU.mult, ALU.add))
                            fresh = False
                        if fresh:
                            link(nc.vector.memset(into, 0.0))

            mean, mean_sq = small[:, 0, :], small[:, 1, :]
            var, dev, inv, tmp = (norm[:, i, :] for i in range(4))
            rs, rs_mean = norm[:, 4, :], norm[:, 5, :]

            def take_stats(loop, turn):
                for i, per in enumerate(BATCHES):
                    at = SPS * turn + sum(BATCHES[:i])
                    for n in range(at, at + per):
                        dve.wait_ge(loaded[n % SLOTS], loop * 32 + (n // SLOTS + 1) * 16)
                    tiles = tiles_of(at % SLOTS, per)
                    for g in range(G):
                        ins = nc.vector.bn_stats(stats[:, g, :], tiles[:, :, g * CG:(g + 1) * CG])
                    link(ins)
                    if i == 0 and not (isinstance(loop, int) and loop == 0 and turn == 0):
                        dve.wait_ge(moments_summed, loop * TURNS + turn)
                    by_half = stats[:, :, :].rearrange("p g (t s) -> p g t s", t=2)
                    half_mean, half_m2 = by_half[:, :, :, 1], by_half[:, :, :, 2]
                    nc.vector.tensor_scalar(moments[:, i, 0], half_mean, float(per), None, ALU.mult)
                    link(nc.vector.scalar_tensor_tensor(moments[:, i, 1], half_mean, float(per), half_mean,
                                                        ALU.mult, ALU.mult))
                    nc.vector.scalar_tensor_tensor(moments[:, i, 1], half_m2, 1.0 / (QN * CG // 2),
                                                   moments[:, i, 1], ALU.mult, ALU.add).then_inc(stats_taken, 1)
                    dve.wait_ge(stats_taken, (loop * TURNS + turn) * len(BATCHES) + i + 1)

            def fold_norm(loop, turn):
                dve.wait_ge(moments_summed, loop * TURNS + turn + 1)
                link(nc.vector.tensor_reduce(small[:, :, :], misc_ps[:, 0:4 * G].rearrange("p (m g t) -> p m g t", m=2, t=2),
                                             AX.X, ALU.add))
                link(nc.vector.tensor_tensor(tmp, mean, mean, ALU.mult))
                link(nc.vector.tensor_tensor(var, mean_sq, tmp, ALU.subtract))
                nc.vector.tensor_scalar(var, var, 0.0, GN_EPS, ALU.max, ALU.add).then_inc(variance_ready, 1)
                dve.wait_ge(deviation_ready, loop * TURNS + turn + 1)
                link(nc.vector.reciprocal(inv, dev))
                link(nc.vector.tensor_tensor(tmp, inv, inv, ALU.mult))
                link(nc.vector.tensor_tensor(tmp, tmp, var, ALU.mult))
                link(nc.vector.tensor_scalar(tmp, tmp, -0.5, 1.5, ALU.mult, ALU.add))
                link(nc.vector.tensor_tensor(rs, inv, tmp, ALU.mult))
                link(nc.vector.tensor_tensor(rs_mean, rs, mean, ALU.mult))
                link(nc.vector.tensor_tensor(picked, rs.unsqueeze(1).broadcast_to([P, KB, G]), group_of[:, :, :], ALU.mult))
                link(nc.vector.tensor_reduce(of_channel[:, :], picked, AX.X, ALU.add))
                if not (isinstance(loop, int) and loop == 0):
                    dve.wait_ge(xc_copied, loop * TURNS + turn - TURNS + 1)
                link(nc.vector.scalar_tensor_tensor(tmp, rs_mean, 1.0, group_sum[:, :], ALU.mult, ALU.mult,
                                                    accum_out=sums[:, 0:1]))
                link(nc.vector.tensor_tensor(bias_1[:, 1 + turn:2 + turn], bias_1[:, 0:1], sums[:, 0:1], ALU.subtract))
                for p in range(2):
                    ins = nc.vector.tensor_tensor(w1[turn][:, :, p, p * R:(p + 1) * R], w1T[:, :, :],
                                                  of_channel[:, :].unsqueeze(2).broadcast_to([P, KB, R]), ALU.mult)
                ins.then_inc(w1_ready, 1)

            for turn in range(TURNS):
                take_stats(0, turn)
                if turn == 0:
                    lay_out_w1()
                fold_norm(0, turn)
            start = done[0]
            LINKS = TURNS * (MOMENT_OPS * len(BATCHES) + FOLD_OPS)
            with dve.Fori(1, LOOPS) as loop:
                base[0] = (loop - 1) * LINKS
                for turn in range(TURNS):
                    take_stats(loop, turn)
                    fold_norm(loop, turn)
            assert done[0] - start == LINKS, done[0] - start
            base[0] = (LOOPS - 2) * LINKS
            take_stats(LOOPS, 0)
            fold_norm(LOOPS, 0)

            nc.vector.memset(small[:, 0, 0:1], 0.0).then_inc(high_free, 1)
            nc.vector.memset(all_one[:, :].bitcast(F32), 1.0)
            link(nc.vector.memset(spread[:, :, :, :].bitcast(F32), 0.0))
            for q in range(QN):
                own = ident[:, 2 * R * q:2 * R * (q + 1)]
                for part in range(4):
                    nc.vector.tensor_copy(spread[:, q, part // 2, 2 * R * part:2 * R * (part + 1)], own)
            dve.wait_ge(wl_in, NH * 16)
            expert_taps()
            dve.wait_ge(late_weights_in, (4 + 2 * NH) * 16)
            nc.vector.tensor_copy(w2_rep[:, :, :].rearrange("p k (n r) -> p k n r", n=NH),
                                  w2_raw[:, :, :].unsqueeze(2).broadcast_to([P, KB, NH, R])).then_inc(w2_replicated, 1)
            link(nc.vector.tensor_copy(b2[:, :], b2_raw[:, :]))
            nc.vector.tensor_tensor(b2[32:64, :], b2_raw[32:64, :], b2[32:64, :].bitcast(F32), ALU.subtract)
            dve.wait_ge(masks_ready, 1)
            for p in range(2):
                for part in range(2):
                    link(nc.vector.tensor_tensor(row_kind[:, 2 * p + part:2 * p + part + 1],
                                                 masks[:, SAME, 2 * part + p, 0:1], masks[:, SAME, 4 + 2 * part + p, 0:1], ALU.add))
            logits, rank, neg_max, expo, gate_of = gate[:, 0, :], gate[:, 1, :], gate[:, 2, 0:1], gate[:, 3, :], gate[:, 4, :]
            dve.wait_ge(logits_done, 1)
            link(nc.vector.scalar_tensor_tensor(logits, misc_ps[0:B, 0:E], 1.0 / (HH * WW), gate_b[:, :], ALU.mult, ALU.add))
            link(nc.vector.tensor_reduce(neg_max, logits, AX.X, ALU.max, negate=True))
            nc.vector.memset(rank, 0.0).then_inc(logits_max, 1)
            for j in range(E):
                dve.wait_ge(logits_max, 1)
                link(nc.vector.scalar_tensor_tensor(rank, logits, logits[:, j:j + 1], rank, ALU.is_lt, ALU.add))
                if j + 1 < E:
                    link(nc.vector.scalar_tensor_tensor(rank[:, j + 1:E], logits[:, j + 1:E], logits[:, j:j + 1],
                                                        rank[:, j + 1:E], ALU.is_equal, ALU.add))
            link(nc.vector.tensor_scalar(rank, rank, 1.5, None, ALU.is_lt))
            dve.wait_ge(logits_exp, 1)
            link(nc.vector.tensor_tensor(expo, expo, rank, ALU.mult))
            link(nc.vector.tensor_reduce(gate[:, 5, 0:1], expo, AX.X, ALU.add))
            link(nc.vector.reciprocal(gate[:, 6, 0:1], gate[:, 5, 0:1]))
            link(nc.vector.tensor_scalar(gate_of, expo, gate[:, 6, 0:1], None, ALU.mult))
            nc.vector.tensor_tensor(gate_diag[:, :, :], gate_of.unsqueeze(1).broadcast_to([B, B, E]),
                                    ident[0:B, 0:B].unsqueeze(2).broadcast_to([B, B, E]), ALU.mult).then_inc(gate_rows, 1)
            dve.wait_ge(gates_spread, 1)
            table = misc_ps[:, 64:64 + B * E].rearrange("p (e b) -> p b e", e=E)
            whole = float(P * SPS * 2)
            nc.vector.tensor_scalar(gates[:, 0, :], table[:, B - 1, :], whole, None, ALU.mult)
            link(nc.vector.tensor_scalar(gates[:, 1:B, :], table[:, 0:B - 1, :], whole, None, ALU.mult))
            link(nc.vector.tensor_reduce(bias_es[:, :], gates[:, :, :], AX.X, ALU.add))
            link(nc.vector.tensor_scalar(bias_es[:, :], bias_es[:, :], bias_l[:, 0:1], None, ALU.mult))
            nc.vector.memset(small[:, 0, 0:1], 0.0).then_inc(gates_ready, 1)

            def make_bands(order):
                flat = "p a x r -> p (a x r)"
                all_e = taps[:, :, :, :].rearrange(flat)
                for e in range(E):
                    g, of_e = gates[:, order, e:e + 1], experts[:, e].rearrange(flat)
                    if e == 0:
                        link(nc.vector.tensor_scalar(all_e, of_e, g, None, ALU.mult))
                    else:
                        link(nc.vector.scalar_tensor_tensor(all_e, of_e, g, all_e, ALU.mult, ALU.add))
                for m in MAT_ORDER:
                    full = [P, NT, NH, R]
                    nc.vector.tensor_tensor(band[:, m], taps[:, MAT_ROW_TAP[m]].unsqueeze(2).broadcast_to(full),
                                            masks[:, MAT_MASK[m]].unsqueeze(1).broadcast_to(full),
                                            ALU.mult).then_inc(band_ready, 1)

            make_bands(0)
            dve.wait_ge(w2_transposed, 1)
            link(nc.vector.tensor_copy(w2_hi[:, :], flat_ps[:, 0, 0:D]))
            link(nc.vector.tensor_tensor(w2_lo[:, :], flat_ps[:, 0, 0:D], w2_hi[:, :].bitcast(F32), ALU.subtract))
            w2_part = w2_rep[:, :, :].rearrange("p k m -> p (k m)")
            for p in range(2):
                link(nc.vector.tensor_scalar(w2_part, w2_lo[:, :], row_kind[:, 2 * p + 1:2 * p + 2], None, ALU.mult))
                ins = nc.vector.scalar_tensor_tensor(w2[:, p, :], w2_hi[:, :].bitcast(F32), row_kind[:, 2 * p:2 * p + 1],
                                                     w2_part, ALU.mult, ALU.add)
                if p == 0:
                    link(ins)
            ins.then_inc(w2_ready, 1)

            def low_half(order):
                dve.wait_ge(hi_ready, order + 1)
                nc.vector.scalar_tensor_tensor(es_lo[:, :], img_ps[:, :], bias_es[:, bass.ds(order, 1)],
                                               es_hi[:, :].bitcast(F32), ALU.add, ALU.subtract).then_inc(lo_ready, 1)

            def add_sample(order, more):
                if more:
                    dve.wait_ge(conv_done, order + 1)
                    make_bands(order + 1)
                for i in range(SPS):
                    if more and i == SPS - 1:
                        low_half(order + 1)
                    uses = -(-(B * SPS - i) // SLOTS)
                    dve.wait_ge(loaded[i], (order + uses) * 16)
                    for q in range(QN):
                        n = i * QN + q
                        dve.wait_ge(expanded, order * TILES + n + 1)
                        nc.vector.tensor_tensor(slot(i)[:, q, :], slot(i)[:, q, :], add_ps[:, n % 2, :],
                                                ALU.add).then_inc(added, 1)

            low_half(0)
            start, before = done[0], base[0]
            with dve.Fori(0, B - 1) as order:
                base[0] = before + order * E
                add_sample(order, True)
            assert done[0] - start == E
            base[0] = before + (B - 2) * E
            add_sample(B - 1, False)


_INPUTS = ["x", "L0_conv_conv1_w", "L0_conv_conv1_b", "L0_conv_convl_w", "L0_conv_convl_b",
           "L0_conv_conv2_w", "L0_conv_conv2_b", "L0_conv_H_w", "L0_conv_H_b"]


def kernel(**inputs):
    import numpy as np
    import concourse.bacc as bacc
    from concourse import mybir as mb
    from concourse.bass_utils import run_bass_kernel_spmd

    nc = bacc.Bacc("TRN2", target_bir_lowering=False, num_devices=1)
    arrays, args = {}, []
    for name in _INPUTS:
        a = np.ascontiguousarray(inputs[name])
        arrays[f"in_{name}"] = a
        args.append(nc.dram_tensor(f"in_{name}", a.shape, mb.dt.from_np(a.dtype), kind="ExternalInput").ap())
    args.append(nc.dram_tensor("out", (B, HH, WW, D), F32, kind="ExternalOutput").ap())
    program(nc, *args)
    result = run_bass_kernel_spmd(nc, [arrays], core_ids=[0])
    return result.results[0]["out"]
```

```python
from contextlib import ExitStack

import concourse.bass as bass
from concourse import mybir

F32 = mybir.dt.float32
BF16 = mybir.dt.bfloat16
F32R = mybir.dt.float32r
ALU = mybir.AluOpType
ACT = mybir.ActivationFunctionType
AX = mybir.AxisListType

P = 128
B, HH, WW, D = 16, 64, 64, 768
R, E = 16, 4
G = 32
CG = D // G
KB = D // P
NH = P // R
NB = HH // NH
PIX = NB * WW
QN = 4
TILES = HH * WW // P
SPS = TILES // QN
CHUNKS = SPS // 2
SLOTS = 12
LOW = 8
TURNS = 3
LOOPS = (B - 1) // TURNS
STEPS = CHUNKS * KB
XT_PS = 3
XT = 6
LEAD = KB
GV = G - 2
STATS_BUFS = 2
HALF = 2 * QN * CG // 2
SUMS_AT = [4, 9, 14, 19]
SCALAR_AT = [at + g for at in (1, 6, 11, 15) for g in range(G - GV)]
FOLD_OPS = 9
AHEAD_SUM = 4
AHEAD_DEVIATION = 3
AHEAD = AHEAD_SUM + AHEAD_DEVIATION + FOLD_OPS - 1
WEIGHTS_AFTER = 4
GN_EPS = 1e-5
LEFT, MID, RIGHT, LEFT_EDGE, RIGHT_EDGE = range(5)
NT = 5
UP, HERE, DOWN, FROM_ABOVE, FROM_BELOW, TOP, BOTTOM = range(7)
MAT_ROW_TAP = [LEFT, MID, RIGHT, LEFT, RIGHT, LEFT_EDGE, RIGHT_EDGE]
SAME, ABOVE, BELOW, FIRST, LAST = range(5)
MAT_MASK = [SAME, SAME, SAME, ABOVE, BELOW, FIRST, LAST]


def resize_taps():
    coef = []
    for e in range(E):
        f = 2 ** e
        sampled = [0] if f == 1 else [f // 2 - 1, f // 2]
        of_expert = []
        for d in (-1, 0, 1):
            inner = {-1: 0.0, 0: 0.0, 1: 0.0}
            first = last = 0.0
            for k in sampled:
                at = (k + d + 0.5) / f - 0.5
                low = int(at // 1)
                for offset, part in ((low, 1 - (at - low)), (low + 1, at - low)):
                    part /= len(sampled)
                    if not part:
                        continue
                    inner[offset] += part
                    if k + d >= 0 and offset <= 0:
                        first += part
                    if k + d < f and offset >= 0:
                        last += part
            of_expert.append([inner[-1], inner[0], inner[1], first - inner[0], last - inner[0]])
        coef.append(of_expert)
    return coef


def slot_place(i):
    return (i // 2) % 2, 2 * (i // 4) + i % 2


def column_ranges(ax):
    return {LEFT: (slice(1, WW), slice(0, WW - 1)), MID: (slice(0, WW), slice(0, WW)),
            RIGHT: (slice(0, WW - 1), slice(1, WW)), LEFT_EDGE: (slice(0, 1), slice(0, 1)),
            RIGHT_EDGE: (slice(WW - 1, WW), slice(WW - 1, WW))}[ax]


def blk_ranges(m):
    return {UP: (slice(1, NB), slice(0, NB - 1)), HERE: (slice(0, NB), slice(0, NB)),
            DOWN: (slice(0, NB - 1), slice(1, NB)), FROM_ABOVE: (slice(0, 1), slice(NB - 1, NB)),
            FROM_BELOW: (slice(NB - 1, NB), slice(0, 1)), TOP: (slice(0, 1), slice(0, 1)),
            BOTTOM: (slice(NB - 1, NB), slice(NB - 1, NB))}[m]


MAT_ORDER = [HERE, UP, DOWN, FROM_ABOVE, FROM_BELOW, TOP, BOTTOM]
MATS_AT = 2
MATS_BEFORE = [MAT_ORDER[:1], MAT_ORDER[1:3], MAT_ORDER[3:5], MAT_ORDER[5:]]
CONV = [(m, a) for m in MAT_ORDER for a in (MID, LEFT, RIGHT, LEFT_EDGE, RIGHT_EDGE)]


def program(nc, x, conv1_w, conv1_b, convl_w, convl_b, conv2_w, conv2_b, H_w, H_b, out):
    slots_of = "b (q p j bb) w c -> b p j (bb w) q c"
    x_v = x.rearrange(slots_of, q=QN, p=2, j=4, bb=2)
    out_v = out.rearrange(slots_of, q=QN, p=2, j=4, bb=2)
    coef = resize_taps()

    ctx = ExitStack()
    scratch = ExitStack()
    with ctx:
        def sb(name, shape, dt=F32, stack=ctx):
            return stack.enter_context(nc.sbuf_tensor(name, shape, dt))

        def sem(name):
            return ctx.enter_context(nc.semaphore(name))

        x_low = sb("x_low", [P, LOW, QN, D])
        xc = sb("xc", [P, B, PIX])
        ident = sb("ident", [P, P])
        pooled = sb("pooled", [P, B])
        small = sb("small", [P, 3, G])
        x_high = sb("x_high", [P, SLOTS - LOW, QN, D], stack=scratch)
        xT = sb("xT", [P, XT, QN, 2 * P], stack=scratch)
        unread_copy = sb("unread_copy", [P, 2 * QN, CG], BF16, stack=scratch)
        w1T = sb("w1T", [P, KB, R], stack=scratch)
        w1_first = sb("w1_first", [P, KB, 2, 2 * R], stack=scratch)
        group_sum = sb("group_sum", [P, G], stack=scratch)
        group_of = sb("group_of", [P, 2, KB // 2, G // 2], stack=scratch)
        picked = sb("picked", [P, 2, KB // 2, G // 2], stack=scratch)
        stats = sb("stats", [P, STATS_BUFS, G, 6], stack=scratch)
        ones = sb("ones", [P, P], stack=scratch)
        norm = sb("norm", [P, 6, G], stack=scratch)
        of_channel = sb("of_channel", [P, KB], stack=scratch)
        bias_1 = sb("bias_1", [P, 1 + TURNS], stack=scratch)
        sums = sb("sums", [P, 2], stack=scratch)
        unread_squares = xc[:, 0, KB * 4 * R:KB * 4 * R + 2 * QN * CG // 2].bitcast(BF16).rearrange("p (s c) -> p s c", c=CG)
        w1 = [w1_first] + [xc[:, at, 0:KB * 4 * R].rearrange("p (k n r) -> p k n r", k=KB, n=2) for at in (B - 1, 0)]
        w1_rep = x_high[:, SLOTS - LOW - 1, 0, :]
        gate = xT[0:B, 0, 0, 0:8 * E].rearrange("b (i e) -> b i e", i=8)
        gate_diag = xT[0:B, 1, 0, 0:B * E].rearrange("b (s e) -> b s e", s=B)
        scratch.close()
        masks = sb("masks", [P, 5, NH, R])
        experts = sb("experts", [P, E, NT, NT, R])
        gates = sb("gates", [P, B, E])
        bias_l = sb("bias_l", [P, 1])
        bias_es = sb("bias_es", [P, B])
        gate_w = sb("gate_w", [P, E])
        gate_b = sb("gate_b", [R, E])
        wl_raw = sb("wl_raw", [P, R, 9])
        rows_of = sb("rows_of", [P, NT, 3, R])
        spread = sb("spread", [P, QN, 2, P], F32R)
        w2 = sb("w2", [P, 2, D], F32R)
        b2 = sb("b2", [P, D], F32R)
        all_one = sb("all_one", [P, P], F32R)
        w2_raw = sb("w2_raw", [P, KB, R])
        row_kind = sb("row_kind", [P, 4])
        w2_rep = sb("w2_rep", [P, KB, P])
        w2_hi = sb("w2_hi", [P, D], F32R)
        w2_lo = sb("w2_lo", [P, D])
        b2_raw = sb("b2_raw", [P, D])
        taps = sb("taps", [P, NT, NT, R])
        es_hi = sb("es_hi", [P, PIX], F32R)
        es_lo = sb("es_lo", [P, PIX], F32R)
        band = sb("band", [P, 7, NT, NH, R])
        es4 = sb("es4", [P, QN, PIX], F32R)

        xT_ps = ctx.enter_context(nc.psum_tensor("xT_ps", [P, XT_PS, QN, 2 * P], F32))
        img_ps = ctx.enter_context(nc.psum_tensor("img_ps", [P, PIX], F32))
        misc_ps = ctx.enter_context(nc.psum_tensor("misc_ps", [P, 512], F32))
        flat_ps = xT_ps[:, :, :, :].rearrange("p n q c -> p n (q c)")
        add_ps = flat_ps[:, 0:2, 0:D]
        spread_ps = flat_ps[:, 2, :].rearrange("p (n c) -> p n c", n=2)
        w1_ps = [(img_ps if k < 4 else misc_ps)[:, k % 4 * P:(k % 4 + 1) * P] for k in range(KB)]
        img_v = img_ps[:, :].rearrange("p (k w) -> p k w", w=WW)
        xc_v = xc[:, :, :].rearrange("p b (k w) -> p b k w", w=WW)

        def slot(n):
            return x_low[:, n] if n < LOW else x_high[:, n - LOW]

        def tiles_of(n, count):
            part = x_low[:, n:n + count] if n < LOW else x_high[:, n - LOW:n - LOW + count]
            return part.rearrange("p s q c -> p (s q) c")

        loaded = [sem(f"loaded{n}") for n in range(SLOTS)]
        weights_in = sem("weights_in")
        consts_ready = sem("consts_ready")
        w1_laid_out = sem("w1_laid_out")
        w1_in_psum = sem("w1_in_psum")
        stats_taken = sem("stats_taken")
        scalar_stats = sem("scalar_stats")
        transposed = sem("transposed")
        xT_copied = sem("xT_copied")
        projected = sem("projected")
        moments_summed = sem("moments_summed")
        variance_ready = sem("variance_ready")
        deviation_ready = sem("deviation_ready")
        w1_ready = sem("w1_ready")
        xc_copied = sem("xc_copied")
        vector_step = sem("vector_step")
        pool_step = sem("pool_step")
        logits_done = sem("logits_done")
        logits_max = sem("logits_max")
        logits_exp = sem("logits_exp")
        gate_rows = sem("gate_rows")
        gates_spread = sem("gates_spread")
        masks_ready = sem("masks_ready")
        bias_zero = sem("bias_zero")
        high_free = sem("high_free")
        wl_in = sem("wl_in")
        late_weights_in = sem("late_weights_in")
        gates_ready = sem("gates_ready")
        w2_replicated = sem("w2_replicated")
        w2_transposed = sem("w2_transposed")
        w2_ready = sem("w2_ready")
        band_ready = sem("band_ready")
        conv_done = sem("conv_done")
        hi_ready = sem("hi_ready")
        lo_ready = sem("lo_ready")
        spread_done = sem("spread_done")
        es4_ready = sem("es4_ready")
        expanded = sem("expanded")
        added = sem("added")
        stored = [sem(f"stored{n}") for n in range(LOW)]

        block = ctx.enter_context(nc.Block())

        @block.sync
        def _(sp):
            def load(sample, i, n):
                p, j = slot_place(i)
                sp.dma_start(slot(n), x_v[sample, p, j]).then_inc(loaded[n], 16)

            def load_sample(loop, turn, first):
                for i in range(SPS):
                    at = SPS * turn + i
                    if not (first and at < SLOTS):
                        if i % 2 == 0:
                            last = (at - SLOTS) // 2 + 1
                            sp.wait_ge(transposed, loop * (TURNS * STEPS) + last * KB)
                    if first and at == WEIGHTS_AFTER:
                        load_weights()
                    if first and at == SLOTS - 1:
                        sp.wait_ge(w1_laid_out, 1)
                    load(loop * TURNS + turn, i, at % SLOTS)

            def load_weights():
                for h in range(NH):
                    rows = slice(R * h, R * h + R)
                    sp.dma_start(w1_rep[rows, :], conv1_w.rearrange("r c y x -> r (c y x)")).then_inc(weights_in, 16)
                    sp.dma_start(bias_1[rows, 0:1], conv1_b.unsqueeze(1)).then_inc(weights_in, 16)

            def load_late_weights():
                sp.wait_ge(high_free, 1)
                for h in range(NH):
                    sp.dma_start(wl_raw[R * h:R * h + R, :, :], convl_w.rearrange("o i y x -> i o (y x)")
                                 ).then_inc(wl_in, 16)
                sp.wait_ge(bias_zero, 1)
                for row in (0, 32):
                    sp.dma_start(b2_raw[row:row + 1, :], conv2_b.unsqueeze(0)).then_inc(late_weights_in, 16)
                sp.dma_start(w2_raw[:, :, :], conv2_w.rearrange("(k c) r y x -> c k (r y x)", k=KB)
                             ).then_inc(late_weights_in, 16)
                sp.dma_start(gate_b[:, :], H_b.partition_broadcast(R)).then_inc(late_weights_in, 16)
                for h in range(NH):
                    rows = slice(R * h, R * h + R)
                    sp.dma_start(bias_l[rows, :], convl_b.unsqueeze(1)).then_inc(late_weights_in, 16)
                    sp.dma_start(gate_w[rows, :], H_w.rearrange("e r -> r e"),
                                 allow_slow_non_contiguous=True).then_inc(late_weights_in, 16)

            for turn in range(TURNS):
                load_sample(0, turn, True)
            with sp.Fori(1, LOOPS) as loop:
                for turn in range(TURNS):
                    load_sample(loop, turn, False)
            load_sample(LOOPS, 0, False)
            load_late_weights()

            def store(order, sample, i):
                p, j = slot_place(i)
                sp.wait_ge(added, order * TILES + (i + 1) * QN)
                sp.dma_start(out_v[sample, p, j], slot(i)).then_inc(stored[i], 16)

            def reload(order, sample, i):
                sp.wait_ge(stored[i], order * 16 + 16)
                load(sample, i, i)

            def store_and_reload(order, sample, following):
                for i in range(SPS):
                    store(order, sample, i)
                    if i >= 2:
                        reload(order, following, i - 2)
                for i in (SPS - 2, SPS - 1):
                    reload(order, following, i)

            store_and_reload(0, B - 1, 0)
            with sp.Fori(1, B - 1) as order:
                store_and_reload(order, order - 1, order)
            for i in range(SPS):
                store(B - 1, B - 2, i)
            for i in range(SPS):
                sp.wait_ge(stored[i], 16 * B)

        @block.gpsimd
        def _(pool):
            done = [0]

            def link(ins):
                done[0] += 1
                ins.then_inc(pool_step, 1)
                pool.wait_ge(pool_step, done[0])

            def keep_where(tile, base, pattern, per_partition):
                link(nc.gpsimd.affine_select(out=tile, in_=tile, compare_op=ALU.is_ge, fill=0.0, base=base,
                                             pattern=pattern, channel_multiplier=per_partition))

            link(nc.gpsimd.memset(ident[:, :], 0.0))
            link(nc.gpsimd.affine_select(out=ident[:, :], in_=ident[:, :], compare_op=ALU.not_equal, fill=1.0,
                                         base=0, pattern=[[-1, P]], channel_multiplier=1))
            link(nc.gpsimd.memset(group_of[:, :, :, :], 1.0))
            keep_where(group_of[:, :, :, :], 0, [[0, 2], [P, KB // 2], [-CG, G // 2]], 1)
            keep_where(group_of[:, :, :, :], CG - 1, [[0, 2], [-P, KB // 2], [CG, G // 2]], -1)
            nc.gpsimd.memset(stats[:, :, GV:G, :], 0.0)
            link(nc.gpsimd.memset(ones[:, :], 1.0 / (P * CHUNKS * 2)))
            for turn in range(TURNS):
                ins = nc.gpsimd.memset(w1[turn][:, :, :, :], 0.0)
            ins.then_inc(consts_ready, 1)

            pool.wait_ge(high_free, 1)
            nc.gpsimd.memset(b2_raw[:, :], 0.0).then_inc(bias_zero, 1)
            link(nc.gpsimd.memset(masks[:, :, :, :], 1.0))
            for kind, shift in ((SAME, 0), (ABOVE, -1), (BELOW, 1), (FIRST, 0), (LAST, 0)):
                keep_where(masks[:, kind], -R * shift, [[-R, NH], [0, R]], 1)
                keep_where(masks[:, kind], R * shift + R - 1, [[R, NH], [0, R]], -1)
            link(nc.gpsimd.memset(masks[:, FIRST, 1:NH], 0.0))
            nc.gpsimd.memset(masks[:, LAST, 0:NH - 1], 0.0).then_inc(masks_ready, 1)

        @block.tensor
        def _(pe):
            pe.wait_ge(consts_ready, 1)

            def transpose_step(loop, turn, step):
                c, k = divmod(step, KB)
                n = turn * STEPS + step
                buf = n % XT_PS
                if k == 0:
                    for s in (2 * c, 2 * c + 1):
                        at = SPS * turn + s
                        pe.wait_ge(loaded[at % SLOTS], loop * 32 + (at // SLOTS + 1) * 16)
                if not (isinstance(loop, int) and loop == 0 and n < XT_PS):
                    pe.wait_ge(xT_copied, loop * (TURNS * STEPS) + n - XT_PS + 1)
                if step == KB - 1:
                    pe.wait_ge(stats_taken, (loop * TURNS + turn) * CHUNKS + 1)
                    pe.wait_ge(scalar_stats, (loop * (TURNS * CHUNKS) + turn * CHUNKS + 1) * 2 * (G - GV))
                for q in range(QN):
                    for half in range(2):
                        last = nc.tensor.transpose(
                            xT_ps[:, buf, q, half * P:(half + 1) * P],
                            slot((SPS * turn + 2 * c + half) % SLOTS)[:, q, k * P:(k + 1) * P], ident[:, :])
                last.then_inc(transposed, 1)

            def project_step(loop, turn, step):
                c, k = divmod(step, KB)
                n = turn * STEPS + step
                pe.wait_ge(xT_copied, loop * (TURNS * STEPS) + n + 1)
                for q in range(QN):
                    last = nc.tensor.matmul(
                        img_ps[32 * q:32 * q + 32, 2 * P * (c // 2):2 * P * (c // 2 + 1)],
                        w1[turn][:, k, c % 2, :], xT[:, n % XT, q, :],
                        start=(c % 2 == 0 and k == 0), stop=(c % 2 == 1 and k == KB - 1))
                last.then_inc(projected, 1)

            def sum_moments(loop, turn, c):
                pe.wait_ge(stats_taken, loop * (TURNS * CHUNKS) + turn * CHUNKS + c + 1)
                pe.wait_ge(scalar_stats, (loop * (TURNS * CHUNKS) + turn * CHUNKS + c + 1) * 2 * (G - GV))
                nc.tensor.matmul(misc_ps[:, 0:6 * G], ones[:, :], stats[:, c % STATS_BUFS].rearrange("p g t -> p (g t)"),
                                 start=(c == 0), stop=(c == CHUNKS - 1)).then_inc(moments_summed, 1)

            def project_sample(loop, turn, more):
                following = (loop, turn + 1) if turn + 1 < TURNS else (loop + 1, 0)
                pe.wait_ge(w1_ready, loop * TURNS + turn + 1)
                for step in range(STEPS):
                    if step + LEAD < STEPS:
                        transpose_step(loop, turn, step + LEAD)
                    elif more:
                        transpose_step(*following, step + LEAD - STEPS)
                    if step == 0 and not (isinstance(loop, int) and loop == 0 and turn == 0):
                        pe.wait_ge(xc_copied, loop * TURNS + turn)
                    project_step(loop, turn, step)
                    if step in SUMS_AT and more:
                        sum_moments(*following, SUMS_AT.index(step))

            for step in range(LEAD):
                transpose_step(0, 0, step)
            pe.wait_ge(weights_in, 2 * NH * 16)
            for k in range(KB):
                last = nc.tensor.transpose(w1_ps[k], w1_rep[:, k * P:(k + 1) * P], ident[:, :])
            last.then_inc(w1_in_psum, 1)
            pe.wait_ge(w1_laid_out, 1)
            for c in range(CHUNKS):
                sum_moments(0, 0, c)
            for turn in range(TURNS):
                project_sample(0, turn, True)
            with pe.Fori(1, LOOPS) as loop:
                for turn in range(TURNS):
                    project_sample(loop, turn, True)
            project_sample(LOOPS, 0, False)

            pe.wait_ge(w2_replicated, 1)
            pe.wait_ge(xc_copied, B)
            for k in range(KB):
                last = nc.tensor.transpose(flat_ps[:, 0, k * P:(k + 1) * P], w2_rep[:, k, :], ident[:, :])
            last.then_inc(w2_transposed, 1)
            nc.tensor.matmul(misc_ps[0:B, 0:E], pooled[:, :], gate_w[:, :], start=True, stop=True).then_inc(logits_done, 1)
            pe.wait_ge(gate_rows, 1)
            nc.tensor.matmul(misc_ps[:, 64:64 + B * E], ones[0:B, :], gate_diag[:, :, :].rearrange("p b e -> p (b e)"),
                             start=True, stop=True).then_inc(gates_spread, 1)

            def conv_part(order, part):
                for m, ax in part:
                    if ax == MID:
                        pe.wait_ge(band_ready, order * 7 + MAT_ORDER.index(m) + 1)
                    blk_out, blk_in = blk_ranges(m)
                    col_out, col_in = column_ranges(ax)
                    last = nc.tensor.matmul(
                        img_v[:, blk_out, col_out], band[:, m, ax].rearrange("p h r -> p (h r)"),
                        xc_v[:, order, blk_in, col_in],
                        start=((m, ax) == CONV[0]), stop=((m, ax) == CONV[-1]))
                return last

            def spread_sample(order):
                pe.wait_ge(hi_ready, order + 1)
                pe.wait_ge(lo_ready, order + 1)
                for q in range(QN):
                    if q >= 2:
                        pe.wait_ge(es4_ready, order * QN + q - 1)
                    nc.tensor.matmul(spread_ps[:, q % 2, :], spread[:, q, 0, :], es_hi[:, :], start=True, stop=False)
                    nc.tensor.matmul(spread_ps[:, q % 2, :], spread[:, q, 1, :], es_lo[:, :],
                                     start=False, stop=True).then_inc(spread_done, 1)

            def expand_slot(order, i):
                p, j = slot_place(i)
                for q in range(QN):
                    n = i * QN + q
                    if i == 0:
                        pe.wait_ge(es4_ready, order * QN + q + 1)
                    if not (isinstance(order, int) and order == 0 and n < 2):
                        pe.wait_ge(added, order * TILES + n - 1)
                    for part in (slice(0, 512), slice(512, D)):
                        nc.tensor.matmul(add_ps[:, n % 2, part], all_one[:, :], b2[:, part], start=True, stop=False)
                        last = nc.tensor.matmul(add_ps[:, n % 2, part], es4[:, q, j * P:(j + 1) * P], w2[:, p, part],
                                                start=False, stop=True)
                    last.then_inc(expanded, 1)

            def expand_sample(order, following):
                for i in range(SPS):
                    expand_slot(order, i)
                    if following is not None and 3 <= i < 7:
                        share = -(-len(CONV) // 4)
                        last = conv_part(following, CONV[(i - 3) * share:(i - 2) * share])
                        if i == 6:
                            last.then_inc(conv_done, 1)

            conv_part(0, CONV).then_inc(conv_done, 1)
            pe.wait_ge(w2_ready, 1)
            spread_sample(0)
            expand_sample(0, 1)
            with pe.Fori(1, B - 1) as order:
                spread_sample(order)
                expand_sample(order, order + 1)
            spread_sample(B - 1)
            expand_sample(B - 1, None)

        @block.scalar
        def _(act):
            def copy_step(loop, turn, step):
                n = turn * STEPS + step
                act.wait_ge(transposed, loop * (TURNS * STEPS) + n + 1)
                if not (isinstance(loop, int) and loop == 0 and n < XT):
                    act.wait_ge(projected, loop * (TURNS * STEPS) + n - XT + 1)
                nc.scalar.copy(xT[:, n % XT], xT_ps[:, n % XT_PS]).then_inc(xT_copied, 1)

            def deviation(loop, turn):
                act.wait_ge(variance_ready, loop * TURNS + turn + 1)
                nc.scalar.activation(norm[:, 1, :], norm[:, 0, :], ACT.Sqrt).then_inc(deviation_ready, 1)

            def scalar_group(loop, turn, c, g):
                if g == GV:
                    for at in (SPS * turn + 2 * c, SPS * turn + 2 * c + 1):
                        act.wait_ge(loaded[at % SLOTS], loop * 32 + (at // SLOTS + 1) * 16)
                    if not (isinstance(loop, int) and loop == 0 and turn == 0 and c < STATS_BUFS):
                        act.wait_ge(moments_summed, loop * (TURNS * CHUNKS) + turn * CHUNKS + c - STATS_BUFS + 1)
                group = tiles_of((SPS * turn + 2 * c) % SLOTS, 2)[:, :, g * CG:(g + 1) * CG]
                before = 2 * (G - GV) * (loop * (TURNS * CHUNKS) + turn * CHUNKS + c) + 2 * (g - GV)
                if not (isinstance(before, int) and before == 0):
                    act.wait_ge(scalar_stats, before)
                nc.scalar.activation(unread_squares, group, ACT.Square,
                                     accum_out=stats[:, c % STATS_BUFS, g, 0:1]).then_inc(scalar_stats, 1)
                nc.scalar.activation(unread_copy[:, :, :], group, ACT.Identity, scale=1.0 / HALF,
                                     accum_out=stats[:, c % STATS_BUFS, g, 1:2]).then_inc(scalar_stats, 1)

            def copy_image(loop, turn, sample, at):
                act.wait_ge(projected, loop * (TURNS * STEPS) + (turn + 1) * STEPS)
                nc.scalar.activation(xc[:, at, :], img_ps[:, :], ACT.Identity, bias=bias_1[:, 1 + turn:2 + turn],
                                     accum_out=pooled[:, bass.ds(sample, 1)]).then_inc(xc_copied, 1)

            def copy_sample(loop, turn):
                following = (loop, turn + 1) if turn + 1 < TURNS else (loop + 1, 0)
                for step in range(STEPS):
                    if step + LEAD < STEPS:
                        copy_step(loop, turn, step + LEAD)
                    else:
                        copy_step(*following, step + LEAD - STEPS)
                    if step in SCALAR_AT:
                        c, g = divmod(SCALAR_AT.index(step), G - GV)
                        scalar_group(*following, c, GV + g)
                    if step == SUMS_AT[-1]:
                        deviation(*following)
                copy_image(loop, turn, loop * TURNS + turn, loop * TURNS + turn + 1)

            act.wait_ge(consts_ready, 1)
            for c in range(CHUNKS):
                for g in range(GV, G):
                    scalar_group(0, 0, c, g)
                if c == 0:
                    for step in range(LEAD):
                        copy_step(0, 0, step)
            deviation(0, 0)
            for turn in range(TURNS):
                copy_sample(0, turn)
            with act.Fori(1, LOOPS) as loop:
                for turn in range(TURNS):
                    copy_sample(loop, turn)
            for step in range(LEAD, STEPS):
                copy_step(LOOPS, 0, step)
            copy_image(LOOPS, 0, B - 1, 0)

            act.wait_ge(logits_max, 1)
            nc.scalar.activation(gate[:, 3, :], gate[:, 0, :], ACT.Exp, bias=gate[:, 2, 0:1]).then_inc(logits_exp, 1)

            def split_sample(order):
                act.wait_ge(conv_done, order + 1)
                nc.scalar.activation(es_hi[:, :], img_ps[:, :], ACT.Identity,
                                     bias=bias_es[:, bass.ds(order, 1)]).then_inc(hi_ready, 1)
                for q in range(QN):
                    act.wait_ge(spread_done, order * QN + q + 1)
                    nc.scalar.copy(es4[:, q, :], spread_ps[:, q % 2, :]).then_inc(es4_ready, 1)

            act.wait_ge(gates_ready, 1)
            with act.Fori(0, B) as order:
                split_sample(order)

        @block.vector
        def _(dve):
            done = [0]
            base = [0]

            def link(ins):
                done[0] += 1
                ins.then_inc(vector_step, 1)
                dve.wait_ge(vector_step, base[0] + done[0])

            dve.wait_ge(consts_ready, 1)

            def lay_out_w1():
                dve.wait_ge(w1_in_psum, 1)
                for k in range(KB):
                    nc.vector.tensor_copy(w1T[:, k, :], w1_ps[k][:, 0:R])
                nc.vector.tensor_reduce(group_sum[:, :], w1_rep.rearrange("p (g c) -> p g c", g=G), AX.X,
                                        ALU.add).then_inc(w1_laid_out, 1)

            def expert_taps():
                wl = wl_raw[:, :, :].rearrange("p o (y x) -> p y x o", y=3)
                for e in range(E):
                    for a in range(NT):
                        fresh = True
                        for d in range(3):
                            c = coef[e][d][a]
                            if c == 0.0:
                                continue
                            if fresh:
                                link(nc.vector.tensor_scalar(rows_of[:, a], wl[:, d], c, None, ALU.mult))
                            else:
                                link(nc.vector.scalar_tensor_tensor(rows_of[:, a], wl[:, d], c, rows_of[:, a],
                                                                    ALU.mult, ALU.add))
                            fresh = False
                        if fresh:
                            link(nc.vector.memset(rows_of[:, a], 0.0))
                    for a in range(NT):
                        fresh = True
                        into = experts[:, e, :, a, :]
                        for d in range(3):
                            c = coef[e][d][a]
                            if c == 0.0:
                                continue
                            if fresh:
                                link(nc.vector.tensor_scalar(into, rows_of[:, :, d, :], c, None, ALU.mult))
                            else:
                                link(nc.vector.scalar_tensor_tensor(into, rows_of[:, :, d, :], c, into,
                                                                    ALU.mult, ALU.add))
                            fresh = False
                        if fresh:
                            link(nc.vector.memset(into, 0.0))

            sq_of_mean, mean, mean_m2 = small[:, 0, :], small[:, 1, :], small[:, 2, :]
            var, dev, inv, tmp = (norm[:, i, :] for i in range(4))
            rs, rs_mean = norm[:, 4, :], norm[:, 5, :]

            def take_groups(loop, turn, c, groups):
                if groups.start == 0:
                    for at in (SPS * turn + 2 * c, SPS * turn + 2 * c + 1):
                        dve.wait_ge(loaded[at % SLOTS], loop * 32 + (at // SLOTS + 1) * 16)
                    if not (isinstance(loop, int) and loop == 0 and turn == 0 and c < STATS_BUFS):
                        dve.wait_ge(moments_summed, loop * (TURNS * CHUNKS) + turn * CHUNKS + c - STATS_BUFS + 1)
                tiles = tiles_of((SPS * turn + 2 * c) % SLOTS, 2)
                for g in groups:
                    ins = nc.vector.bn_stats(stats[:, c % STATS_BUFS, g, :], tiles[:, :, g * CG:(g + 1) * CG])
                return ins

            def take_stats(loop, turn, ahead):
                for c in range(CHUNKS):
                    if c == STATS_BUFS and isinstance(loop, int) and loop == 0 and turn == 0:
                        lay_out_w1()
                    link(take_groups(loop, turn, c, range(ahead if c == 0 else 0, GV)))
                    by_half = stats[:, c % STATS_BUFS, 0:GV].rearrange("p g (t s) -> p g t s", t=2)
                    nc.vector.scalar_tensor_tensor(by_half[:, :, :, 0], by_half[:, :, :, 1], float(HALF),
                                                   by_half[:, :, :, 1], ALU.mult, ALU.mult).then_inc(stats_taken, 1)

            def fold_norm(loop, turn, following):
                taken = [0]

                def meanwhile(count):
                    if following:
                        take_groups(*following, 0, range(taken[0], taken[0] + count))
                        taken[0] += count

                def link_over(ins):
                    done[0] += 1
                    ins.then_inc(vector_step, 1)
                    meanwhile(1)
                    dve.wait_ge(vector_step, base[0] + done[0])

                meanwhile(AHEAD_SUM)
                dve.wait_ge(moments_summed, loop * (TURNS * CHUNKS) + (turn + 1) * CHUNKS)
                link_over(nc.vector.tensor_reduce(small[:, :, :], misc_ps[:, 0:6 * G].rearrange("p (g t s) -> p s g t", t=2, s=3),
                                                  AX.X, ALU.add))
                nc.vector.tensor_tensor(tmp, mean, mean, ALU.mult)
                link_over(nc.vector.tensor_tensor(var, sq_of_mean, mean_m2, ALU.add))
                link_over(nc.vector.scalar_tensor_tensor(var, var, 1.0 / HALF, tmp, ALU.mult, ALU.subtract))
                nc.vector.tensor_scalar(var, var, 0.0, GN_EPS, ALU.max, ALU.add).then_inc(variance_ready, 1)
                meanwhile(AHEAD_DEVIATION)
                dve.wait_ge(deviation_ready, loop * TURNS + turn + 1)
                link_over(nc.vector.reciprocal(inv, dev))
                link_over(nc.vector.tensor_tensor(tmp, inv, inv, ALU.mult))
                link_over(nc.vector.scalar_tensor_tensor(tmp, tmp, -0.5, var, ALU.mult, ALU.mult))
                link_over(nc.vector.scalar_tensor_tensor(rs, tmp, 1.5, inv, ALU.add, ALU.mult))
                nc.vector.tensor_tensor(rs_mean, rs, mean, ALU.mult)
                rs_of_half = rs.rearrange("p (n g) -> p n g", n=2).unsqueeze(2).broadcast_to([P, 2, KB // 2, G // 2])
                link_over(nc.vector.tensor_tensor(picked[:, :, :, :], rs_of_half, group_of[:, :, :, :], ALU.mult))
                assert not following or taken[0] == AHEAD
                if not (isinstance(loop, int) and loop == 0):
                    dve.wait_ge(xc_copied, loop * TURNS + turn - TURNS + 1)
                nc.vector.tensor_reduce(of_channel[:, :], picked[:, :, :, :].rearrange("p n k g -> p (n k) g"), AX.X, ALU.add)
                link(nc.vector.scalar_tensor_tensor(tmp, rs_mean, 1.0, group_sum[:, :], ALU.mult, ALU.mult,
                                                    accum_out=sums[:, 0:1]))
                nc.vector.tensor_tensor(bias_1[:, 1 + turn:2 + turn], bias_1[:, 0:1], sums[:, 0:1], ALU.subtract)
                for p in range(2):
                    ins = nc.vector.tensor_tensor(w1[turn][:, :, p, p * R:(p + 1) * R], w1T[:, :, :],
                                                  of_channel[:, :].unsqueeze(2).broadcast_to([P, KB, R]), ALU.mult)
                ins.then_inc(w1_ready, 1)
                dve.wait_ge(w1_ready, loop * TURNS + turn + 1)

            def next_sample(loop, turn):
                return (loop, turn + 1) if turn + 1 < TURNS else (loop + 1, 0)

            for turn in range(TURNS):
                take_stats(0, turn, AHEAD if turn > 0 else 0)
                fold_norm(0, turn, next_sample(0, turn))
            start = done[0]
            LINKS = TURNS * (CHUNKS + FOLD_OPS)
            with dve.Fori(1, LOOPS) as loop:
                base[0] = (loop - 1) * LINKS
                for turn in range(TURNS):
                    take_stats(loop, turn, AHEAD)
                    fold_norm(loop, turn, next_sample(loop, turn))
            assert done[0] - start == LINKS, done[0] - start
            base[0] = (LOOPS - 2) * LINKS
            take_stats(LOOPS, 0, AHEAD)
            fold_norm(LOOPS, 0, None)

            nc.vector.memset(small[:, 0, 0:1], 0.0).then_inc(high_free, 1)
            nc.vector.memset(all_one[:, :].bitcast(F32), 1.0)
            link(nc.vector.memset(spread[:, :, :, :].bitcast(F32), 0.0))
            for q in range(QN):
                of_quadrant = ident[:, 2 * R * q:2 * R * (q + 1)]
                for part in range(4):
                    nc.vector.tensor_copy(spread[:, q, part // 2, 2 * R * part:2 * R * (part + 1)], of_quadrant)
            dve.wait_ge(wl_in, NH * 16)
            expert_taps()
            dve.wait_ge(late_weights_in, (4 + 2 * NH) * 16)
            nc.vector.tensor_copy(w2_rep[:, :, :].rearrange("p k (n r) -> p k n r", n=NH),
                                  w2_raw[:, :, :].unsqueeze(2).broadcast_to([P, KB, NH, R])).then_inc(w2_replicated, 1)
            link(nc.vector.tensor_copy(b2[:, :], b2_raw[:, :]))
            nc.vector.tensor_tensor(b2[32:64, :], b2_raw[32:64, :], b2[32:64, :].bitcast(F32), ALU.subtract)
            dve.wait_ge(masks_ready, 1)
            for p in range(2):
                for part in range(2):
                    link(nc.vector.tensor_tensor(row_kind[:, 2 * p + part:2 * p + part + 1],
                                                 masks[:, SAME, 2 * part + p, 0:1], masks[:, SAME, 4 + 2 * part + p, 0:1], ALU.add))
            logits, rank, neg_max, expo, gate_of = gate[:, 0, :], gate[:, 1, :], gate[:, 2, 0:1], gate[:, 3, :], gate[:, 4, :]
            dve.wait_ge(logits_done, 1)
            link(nc.vector.scalar_tensor_tensor(logits, misc_ps[0:B, 0:E], 1.0 / (HH * WW), gate_b[:, :], ALU.mult, ALU.add))
            link(nc.vector.tensor_reduce(neg_max, logits, AX.X, ALU.max, negate=True))
            nc.vector.memset(rank, 0.0).then_inc(logits_max, 1)
            for j in range(E):
                dve.wait_ge(logits_max, 1)
                link(nc.vector.scalar_tensor_tensor(rank, logits, logits[:, j:j + 1], rank, ALU.is_lt, ALU.add))
                if j + 1 < E:
                    link(nc.vector.scalar_tensor_tensor(rank[:, j + 1:E], logits[:, j + 1:E], logits[:, j:j + 1],
                                                        rank[:, j + 1:E], ALU.is_equal, ALU.add))
            link(nc.vector.tensor_scalar(rank, rank, 1.5, None, ALU.is_lt))
            dve.wait_ge(logits_exp, 1)
            link(nc.vector.tensor_tensor(expo, expo, rank, ALU.mult))
            link(nc.vector.tensor_reduce(gate[:, 5, 0:1], expo, AX.X, ALU.add))
            link(nc.vector.reciprocal(gate[:, 6, 0:1], gate[:, 5, 0:1]))
            link(nc.vector.tensor_scalar(gate_of, expo, gate[:, 6, 0:1], None, ALU.mult))
            nc.vector.tensor_tensor(gate_diag[:, :, :], gate_of.unsqueeze(1).broadcast_to([B, B, E]),
                                    ident[0:B, 0:B].unsqueeze(2).broadcast_to([B, B, E]), ALU.mult).then_inc(gate_rows, 1)
            dve.wait_ge(gates_spread, 1)
            table = misc_ps[:, 64:64 + B * E].rearrange("p (e b) -> p b e", e=E)
            whole = float(P * CHUNKS * 2)
            nc.vector.tensor_scalar(gates[:, 0, :], table[:, B - 1, :], whole, None, ALU.mult)
            link(nc.vector.tensor_scalar(gates[:, 1:B, :], table[:, 0:B - 1, :], whole, None, ALU.mult))
            link(nc.vector.tensor_reduce(bias_es[:, :], gates[:, :, :], AX.X, ALU.add))
            link(nc.vector.tensor_scalar(bias_es[:, :], bias_es[:, :], bias_l[:, 0:1], None, ALU.mult))
            nc.vector.memset(small[:, 0, 0:1], 0.0).then_inc(gates_ready, 1)

            def weigh_taps(order):
                flat = "p a x r -> p (a x r)"
                all_e = taps[:, :, :, :].rearrange(flat)
                for e in range(E):
                    g, of_e = gates[:, order, e:e + 1], experts[:, e].rearrange(flat)
                    if e == 0:
                        link(nc.vector.tensor_scalar(all_e, of_e, g, None, ALU.mult))
                    else:
                        link(nc.vector.scalar_tensor_tensor(all_e, of_e, g, all_e, ALU.mult, ALU.add))

            def make_bands(mats):
                for m in mats:
                    shape = [P, NT, NH, R]
                    nc.vector.tensor_tensor(band[:, m], taps[:, MAT_ROW_TAP[m]].unsqueeze(2).broadcast_to(shape),
                                            masks[:, MAT_MASK[m]].unsqueeze(1).broadcast_to(shape),
                                            ALU.mult).then_inc(band_ready, 1)

            weigh_taps(0)
            make_bands(MAT_ORDER)
            dve.wait_ge(w2_transposed, 1)
            link(nc.vector.tensor_copy(w2_hi[:, :], flat_ps[:, 0, 0:D]))
            link(nc.vector.tensor_tensor(w2_lo[:, :], flat_ps[:, 0, 0:D], w2_hi[:, :].bitcast(F32), ALU.subtract))
            w2_part = w2_rep[:, :, :].rearrange("p k m -> p (k m)")
            for p in range(2):
                link(nc.vector.tensor_scalar(w2_part, w2_lo[:, :], row_kind[:, 2 * p + 1:2 * p + 2], None, ALU.mult))
                ins = nc.vector.scalar_tensor_tensor(w2[:, p, :], w2_hi[:, :].bitcast(F32), row_kind[:, 2 * p:2 * p + 1],
                                                     w2_part, ALU.mult, ALU.add)
                if p == 0:
                    link(ins)
            ins.then_inc(w2_ready, 1)

            def low_half(order):
                dve.wait_ge(hi_ready, order + 1)
                nc.vector.scalar_tensor_tensor(es_lo[:, :], img_ps[:, :], bias_es[:, bass.ds(order, 1)],
                                               es_hi[:, :].bitcast(F32), ALU.add, ALU.subtract).then_inc(lo_ready, 1)

            def add_sample(order, more):
                for i in range(SPS):
                    if more and i == MATS_AT:
                        dve.wait_ge(conv_done, order + 1)
                        weigh_taps(order + 1)
                    if more and MATS_AT <= i < MATS_AT + len(MATS_BEFORE):
                        make_bands(MATS_BEFORE[i - MATS_AT])
                    if more and i == SPS - 1:
                        low_half(order + 1)
                    uses = -(-(B * SPS - i) // SLOTS)
                    dve.wait_ge(loaded[i], (order + uses) * 16)
                    for q in range(QN):
                        n = i * QN + q
                        dve.wait_ge(expanded, order * TILES + n + 1)
                        nc.vector.tensor_tensor(slot(i)[:, q, :], slot(i)[:, q, :], add_ps[:, n % 2, :],
                                                ALU.add).then_inc(added, 1)

            low_half(0)
            start, before = done[0], base[0]
            with dve.Fori(0, B - 1) as order:
                base[0] = before + order * E
                add_sample(order, True)
            assert done[0] - start == E
            base[0] = before + (B - 2) * E
            add_sample(B - 1, False)


_INPUTS = ["x", "L0_conv_conv1_w", "L0_conv_conv1_b", "L0_conv_convl_w", "L0_conv_convl_b",
           "L0_conv_conv2_w", "L0_conv_conv2_b", "L0_conv_H_w", "L0_conv_H_b"]


def kernel(**inputs):
    import numpy as np
    import concourse.bacc as bacc
    from concourse import mybir as mb
    from concourse.bass_utils import run_bass_kernel_spmd

    nc = bacc.Bacc("TRN2", target_bir_lowering=False, num_devices=1)
    arrays, args = {}, []
    for name in _INPUTS:
        a = np.ascontiguousarray(inputs[name])
        arrays[f"in_{name}"] = a
        args.append(nc.dram_tensor(f"in_{name}", a.shape, mb.dt.from_np(a.dtype), kind="ExternalInput").ap())
    args.append(nc.dram_tensor("out", (B, HH, WW, D), F32, kind="ExternalOutput").ap())
    program(nc, *args)
    result = run_bass_kernel_spmd(nc, [arrays], core_ids=[0])
    return result.results[0]["out"]
```
